# Optimizing a Trainium2 kernel written in Bass

```python
import numpy as np
import jax
import jax.numpy as jnp

def _softmax(x, axis=-1):
    return jax.nn.softmax(x, axis=axis)

def _gelu(x):
    return jax.nn.gelu(x, approximate=True)

def _silu(x):
    return jax.nn.silu(x)

def _sigmoid(x):
    return jax.nn.sigmoid(x)

def _layernorm(x, axis=-1, eps=1e-05):
    m = jnp.mean(x, axis=axis, keepdims=True)
    v = jnp.var(x, axis=axis, keepdims=True)
    return (x - m) / jnp.sqrt(v + eps)

def _scatter_add(tgt, idx, src, axis=0):
    return tgt.at[idx].add(src)

def _segment_sum(src, seg, n):
    return jax.ops.segment_sum(src, seg, n)
kernel_name = 'mk_hybrid_d1_jaxref_r4_cecf50'

def setup_inputs(seed: int=0):
    np.random.seed(seed)
    _w = jnp.asarray

    def _L0_attn_a_setup():
        import jax, jax.numpy as jnp
        import numpy as np
        HIDDEN = 256
        HEADS = 16
        HEAD_DIM = HIDDEN // HEADS
        BLOCK_SIZE = 64
        NUM_GLOBAL = 4
        SCALE = HEAD_DIM ** (-0.5)

        def _block_mask(seq_len):
            i = jnp.arange(seq_len)[:, None]
            j = jnp.arange(seq_len)[None, :]
            half = BLOCK_SIZE // 2
            window = jnp.abs(i - j) <= half
            glob = (i < NUM_GLOBAL) | (j < NUM_GLOBAL)
            return window | glob
        key = jax.random.key(seed)
        ks = jax.random.split(key, 9)
        B, S = (4, 512)
        x = jax.random.normal(ks[0], (B, S, HIDDEN), dtype=jnp.float32)
        std = HIDDEN ** (-0.5)
        Wq = jax.random.normal(ks[1], (HIDDEN, HIDDEN), dtype=jnp.float32) * std
        bq = jnp.zeros((HIDDEN,), jnp.float32)
        Wk = jax.random.normal(ks[2], (HIDDEN, HIDDEN), dtype=jnp.float32) * std
        bk = jnp.zeros((HIDDEN,), jnp.float32)
        Wv = jax.random.normal(ks[3], (HIDDEN, HIDDEN), dtype=jnp.float32) * std
        bv = jnp.zeros((HIDDEN,), jnp.float32)
        Wo = jax.random.normal(ks[4], (HIDDEN, HIDDEN), dtype=jnp.float32) * std
        bo = jnp.zeros((HIDDEN,), jnp.float32)
        return {'x': x, 'Wq': Wq, 'bq': bq, 'Wk': Wk, 'bk': bk, 'Wv': Wv, 'bv': bv, 'Wo': Wo, 'bo': bo}
    _L0_attn_a_in = _L0_attn_a_setup()

    def _L0_attn_b_setup():
        import jax, jax.numpy as jnp
        import numpy as np
        N_HEADS = 16

        def _rope_tables(C, d_head):
            i = jnp.arange(d_head // 2, dtype=jnp.float32)
            theta = jnp.power(10000.0, -2.0 * (i - 1.0) / d_head)
            ang = jnp.arange(C, dtype=jnp.float32)[:, None] * theta[None, :]
            return (jnp.cos(ang), jnp.sin(ang))

        def _rotate(t, cos, sin):
            te, to = (t[..., 0::2], t[..., 1::2])
            re = te * cos - to * sin
            ro = te * sin + to * cos
            return jnp.stack([re, ro], axis=-1).reshape(t.shape)
        key = jax.random.key(seed)
        k1, k2, k3 = jax.random.split(key, 3)
        B, C, D = (2, 512, 256)
        x = jax.random.normal(k1, (B, C, D), dtype=jnp.float32)
        Wqkv = jax.random.normal(k2, (D, 3 * D), dtype=jnp.float32) * 0.02
        Wout = jax.random.normal(k3, (D, D), dtype=jnp.float32) * 0.02
        bout = jnp.zeros((D,), dtype=jnp.float32)
        return {'x': x, 'Wqkv': Wqkv, 'Wout': Wout, 'bout': bout}
    _L0_attn_b_in = _L0_attn_b_setup()

    def _L0_ffn_setup():
        import jax, jax.numpy as jnp
        import numpy as np
        DIM = 256
        HIDDEN = 768
        SCALE = 1.0 / 127.0

        def _dequant(w_int, dtype):
            return w_int.astype(dtype) * jnp.asarray(SCALE, dtype)
        key = jax.random.key(seed)
        k_x, k_g, k_u, k_d = jax.random.split(key, 4)
        x = jax.random.normal(k_x, (4, 512, DIM), dtype=jnp.float32)
        w_gate = jax.random.randint(k_g, (HIDDEN, DIM), -127, 128, dtype=jnp.int32)
        w_up = jax.random.randint(k_u, (HIDDEN, DIM), -127, 128, dtype=jnp.int32)
        w_down = jax.random.randint(k_d, (DIM, HIDDEN), -127, 128, dtype=jnp.int32)
        return {'x': x, 'w_gate': w_gate, 'w_up': w_up, 'w_down': w_down}
    _L0_ffn_in = _L0_ffn_setup()
    _d = {'L0_attn_a_x': _L0_attn_a_in['x'], 'L0_attn_a_Wq': _L0_attn_a_in['Wq'], 'L0_attn_a_bq': _L0_attn_a_in['bq'], 'L0_attn_a_Wk': _L0_attn_a_in['Wk'], 'L0_attn_a_bk': _L0_attn_a_in['bk'], 'L0_attn_a_Wv': _L0_attn_a_in['Wv'], 'L0_attn_a_bv': _L0_attn_a_in['bv'], 'L0_attn_a_Wo': _L0_attn_a_in['Wo'], 'L0_attn_a_bo': _L0_attn_a_in['bo'], 'L0_attn_b_Wqkv': _L0_attn_b_in['Wqkv'], 'L0_attn_b_Wout': _L0_attn_b_in['Wout'], 'L0_attn_b_bout': _L0_attn_b_in['bout'], 'L0_ffn_w_gate': _L0_ffn_in['w_gate'], 'L0_ffn_w_up': _L0_ffn_in['w_up'], 'L0_ffn_w_down': _L0_ffn_in['w_down']}
    _x0 = _d['L0_attn_a_x']
    _d['L0_attn_a_x'] = jax.random.normal(jax.random.fold_in(jax.random.key(seed), 1), (16, 512, 256), dtype=_x0.dtype)
    del _x0
    return _d

def reference(L0_attn_a_x, L0_attn_a_Wq, L0_attn_a_bq, L0_attn_a_Wk, L0_attn_a_bk, L0_attn_a_Wv, L0_attn_a_bv, L0_attn_a_Wo, L0_attn_a_bo, L0_attn_b_Wqkv, L0_attn_b_Wout, L0_attn_b_bout, L0_ffn_w_gate, L0_ffn_w_up, L0_ffn_w_down):

    def _L0_attn_a_ref(x, Wq, bq, Wk, bk, Wv, bv, Wo, bo):
        import jax, jax.numpy as jnp
        import numpy as np
        HIDDEN = 256
        HEADS = 16
        HEAD_DIM = HIDDEN // HEADS
        BLOCK_SIZE = 64
        NUM_GLOBAL = 4
        SCALE = HEAD_DIM ** (-0.5)

        def _block_mask(seq_len):
            i = jnp.arange(seq_len)[:, None]
            j = jnp.arange(seq_len)[None, :]
            half = BLOCK_SIZE // 2
            window = jnp.abs(i - j) <= half
            glob = (i < NUM_GLOBAL) | (j < NUM_GLOBAL)
            return window | glob
        B, S, _ = x.shape

        def proj(W, b):
            y = jnp.einsum('bsd,ed->bse', x, W) + b
            return y.reshape(B, S, HEADS, HEAD_DIM).transpose(0, 2, 1, 3)
        q = proj(Wq, bq)
        k = proj(Wk, bk)
        v = proj(Wv, bv)
        scores = jnp.einsum('bhsd,bhtd->bhst', q, k) * SCALE
        mask = _block_mask(S)
        scores = jnp.where(mask[None, None], scores, -jnp.inf)
        attn = jax.nn.softmax(scores, axis=-1)
        out = jnp.einsum('bhst,bhtd->bhsd', attn, v)
        out = out.transpose(0, 2, 1, 3).reshape(B, S, HIDDEN)
        return jnp.einsum('bsd,ed->bse', out, Wo) + bo

    def _L0_attn_b_ref(x, Wqkv, Wout, bout):
        import jax, jax.numpy as jnp
        import numpy as np
        N_HEADS = 16

        def _rope_tables(C, d_head):
            i = jnp.arange(d_head // 2, dtype=jnp.float32)
            theta = jnp.power(10000.0, -2.0 * (i - 1.0) / d_head)
            ang = jnp.arange(C, dtype=jnp.float32)[:, None] * theta[None, :]
            return (jnp.cos(ang), jnp.sin(ang))

        def _rotate(t, cos, sin):
            te, to = (t[..., 0::2], t[..., 1::2])
            re = te * cos - to * sin
            ro = te * sin + to * cos
            return jnp.stack([re, ro], axis=-1).reshape(t.shape)
        B, C, D = x.shape
        H = N_HEADS
        dh = D // H
        qkv = x @ Wqkv
        q, k, v = jnp.split(qkv, 3, axis=-1)
        q = q.reshape(B, C, H, dh).transpose(0, 2, 1, 3)
        k = k.reshape(B, C, H, dh).transpose(0, 2, 1, 3)
        v = v.reshape(B, C, H, dh).transpose(0, 2, 1, 3)
        cos, sin = _rope_tables(C, dh)
        q_rot = _rotate(q, cos, sin)
        k_rot = _rotate(k, cos, sin)
        scale = 1.0 / jnp.sqrt(jnp.asarray(dh, dtype=x.dtype))
        num = jnp.exp(jnp.einsum('bhqd,bhkd->bhqk', q_rot, k_rot) * scale)
        den = jnp.sum(jnp.exp(jnp.einsum('bhqd,bhkd->bhqk', q, k) * scale), axis=-1, keepdims=True)
        attn = num / den
        causal = jnp.tril(jnp.ones((C, C), dtype=bool))
        attn = jnp.where(causal[None, None], attn, 0.0)
        y = jnp.einsum('bhqk,bhkd->bhqd', attn, v)
        y = y.transpose(0, 2, 1, 3).reshape(B, C, D)
        return y @ Wout + bout

    def _L0_ffn_ref(x, w_gate, w_up, w_down):
        import jax, jax.numpy as jnp
        import numpy as np
        DIM = 256
        HIDDEN = 768
        SCALE = 1.0 / 127.0

        def _dequant(w_int, dtype):
            return w_int.astype(dtype) * jnp.asarray(SCALE, dtype)
        wg = _dequant(w_gate, x.dtype)
        wu = _dequant(w_up, x.dtype)
        wd = _dequant(w_down, x.dtype)
        gate = jnp.einsum('bsd,hd->bsh', x, wg)
        up = jnp.einsum('bsd,hd->bsh', x, wu)
        h = jax.nn.silu(gate) * up
        return jnp.einsum('bsh,dh->bsd', h, wd)
    x = L0_attn_a_x
    x = x + _L0_attn_a_ref(_layernorm(x, axis=-1), L0_attn_a_Wq, L0_attn_a_bq, L0_attn_a_Wk, L0_attn_a_bk, L0_attn_a_Wv, L0_attn_a_bv, L0_attn_a_Wo, L0_attn_a_bo)
    x = x + _L0_ffn_ref(_layernorm(x, axis=-1), L0_ffn_w_gate, L0_ffn_w_up, L0_ffn_w_down)
    x = x + _L0_attn_b_ref(_layernorm(x, axis=-1), L0_attn_b_Wqkv, L0_attn_b_Wout, L0_attn_b_bout)
    x = x + _L0_ffn_ref(_layernorm(x, axis=-1), L0_ffn_w_gate, L0_ffn_w_up, L0_ffn_w_down)
    return x

_drawn_inputs = setup_inputs


def setup_inputs(seed=0):
    import zlib

    import numpy as np

    out = dict(_drawn_inputs(seed))
    spreads = {'L0_attn_a_bq': (0.0, 0.1),
     'L0_attn_a_bk': (0.0, 0.1),
     'L0_attn_a_bv': (0.0, 0.1),
     'L0_attn_a_bo': (0.0, 0.1),
     'L0_attn_b_bout': (0.0, 0.1)}
    factors = {}
    for name, (base, spread) in spreads.items():
        noise = np.random.default_rng([zlib.crc32(name.encode()), seed]).standard_normal(out[name].shape)
        drawn = base * np.exp(spread * noise) if base else spread * noise
        out[name] = jnp.asarray(drawn.astype(out[name].dtype))
    for name, factor in factors.items():
        out[name] = (out[name] * factor).astype(out[name].dtype)
    return out
```

```python
import numpy as np
import concourse.bass as bass
from concourse import mybir
from concourse.alu_op_type import AluOpType as ALU
from contextlib import ExitStack

F32, F32R = mybir.dt.float32, mybir.dt.float32r
F16, BF16, I32 = mybir.dt.float16, mybir.dt.bfloat16, mybir.dt.int32
ACT = mybir.ActivationFunctionType
AX = mybir.AxisListType

SEQS, S, D = 16, 512, 256
HEADS, DH = 16, 16
HID = 768
P = 128
NT, KT, FT = S // P, D // P, HID // P
GROUPS = 4
PAIRS = HEADS // 2
PACK = HEADS // 2 * S + HEADS * S
HALF, GLOBALS = 32, 4
MASKED = -1e30
EPS = 1e-5
SM_SCALE = float(DH) ** -0.5
DEQUANT = float(np.float32(1.0 / 127.0))
EXACT = 2048.0

WINDOW = [(0, S)] + [(t * P - HALF, min((t + 1) * P + HALF, S)) for t in range(1, NT)]
WIDE = [b - a + (GLOBALS if t else 0) for t, (a, b) in enumerate(WINDOW)]
UNITS_A = [[(0, 0, 0)], [(1, 0, 0)], [(0, 1, 0), (0, 2, WIDE[1])], [(1, 1, 0), (1, 2, WIDE[1])],
           [(0, 3, 0), (1, 3, WIDE[3])]]
UNITS_B = [[(0, 0, 0)], [(1, 0, 0)], [(0, 1, 0), (0, 3, 3 * P)], [(1, 1, 0), (1, 3, 3 * P)],
           [(0, 2, 0), (1, 2, 2 * P)]]
NU = len(UNITS_A)
A_UNITS = B_UNITS = PAIRS * NU
DEN_UNITS = HEADS * NT
SETDMA = 12 * 16
GU = {"OA": GROUPS, "OB": GROUPS, "F": KT + 2 * FT, "PA": KT + 4, "PB": KT + 8}
DU = {"OA": 2, "OB": 1, "F": 1, "PA": 1, "PB": 1}
LINKS = {"OA": 4, "OB": 5, "F": 5, "PA": 5, "PB": 5}
STEPS = [("O", 0), ("O", 1), ("O", 2), ("O", 3), ("O", 4), ("LN", 0)] + \
        [("F", f) for f in range(FT)] + [("F", FT), ("LN", 1)] + [("T", n) for n in range(4)] + [("V", 0)]
AT_TICK = [2, 2, 1, 1, 1, 1, 1, 1, 1, 1, 1, 1, 1, 1, 1, 2]


class Count:

    def __init__(self, const, per=0):
        self.const, self.per = const, per

    def __add__(self, k):
        return Count(self.const + k.const, self.per + k.per) if isinstance(k, Count) else Count(self.const + k, self.per)

    def __mul__(self, k):
        return Count(self.const * k, self.per * k)

    def at(self, turn):
        return self.const + self.per * turn if isinstance(turn, int) or not self.per else turn * self.per + self.const


class Block:

    def __init__(self, name, seq, parity, before):
        self.name, self.seq, self.parity = name, seq, parity
        total = lambda w: sum((before[k] * w[k] for k in before), Count(0))
        self.gu, self.d, self.link = total(GU), total(DU), total(LINKS)
        self.ln = before["F"] + before["PA"] + before["PB"]
        self.o = before["OA"] + before["OB"]
        self.f = before["F"]
        self.p = before["PA"] + before["PB"]
        self.pb = before["PB"]


class Slot:
    def __init__(self, att, blocks, before):
        self.att, self.blocks = att, {}
        for name, seq, parity in blocks:
            self.blocks[name] = Block(name, seq, parity, dict(before))
            before[name] = before[name] + 1
        b = self.blocks
        self.out = b.get("OA") or b.get("OB")
        self.ffn = b.get("F")
        self.proj = b.get("PA") or b.get("PB")

    def steps(self, tick):
        have = {"O": self.out, "F": self.ffn, "T": self.proj, "V": self.proj}
        first = sum(AT_TICK[:tick])
        for kind, n in STEPS[first:first + AT_TICK[tick]]:
            if kind == "LN":
                block = self.ffn if n == 0 else self.proj
            else:
                block = have[kind]
            if block is not None:
                yield kind, n, block


def schedule():
    c = Count
    before = {k: c(0) for k in GU}
    first = [Slot(None, [("PA", c(0), 0)], before), Slot(("A", c(0), 0, None), [("PA", c(1), 1)], before)]
    ev, od, ev2, od2 = c(0, 2), c(1, 2), c(2, 2), c(3, 2)

    def turn(last):
        n = {"OA": c(0, 2), "OB": c(0, 2), "F": c(0, 4), "PB": c(0, 2), "PA": c(2, 2)}
        return [
            Slot(("A", od, 1, ("A", ev)), [("OA", ev, 0), ("F", ev, 0), ("PB", ev, 0)], n),
            Slot(("B", ev, 0, ("A", od)), [("OA", od, 1), ("F", od, 1), ("PB", od, 1)], n),
            Slot(("B", od, 1, ("B", ev)), [("OB", ev, 0), ("F", ev, 0)] + [("PA", ev2, 0)] * (not last), n),
            Slot(None if last else ("A", ev2, 0, ("B", od)),
                 [("OB", od, 1), ("F", od, 1)] + [("PA", od2, 1)] * (not last), n),
        ]

    return first, turn(False), turn(True)


def spread(ap, n):
    return bass.AP(tensor=ap.tensor, offset=ap.offset, ap=[list(x) for x in ap.ap] + [[0, n]])


def build(nc, x_in, Wq, bq, Wk, bk, Wv, bv, Wo, bo, Wqkv, Wout, bout, w_gate, w_up, w_down,
          cos_in, sin_in, masks_in, eye_in, sel_in, sums_in, out):
    nc.disable_value_cache = True
    first, body, tail = schedule()
    ctx = ExitStack()
    with ctx:
        def sb(name, shape, dt):
            return ctx.enter_context(nc.sbuf_tensor(name, shape, dt))

        def sem(name):
            return ctx.enter_context(nc.semaphore(name))

        wa_qk = [sb(f"wa_qk{i}", [P, KT, 2 * D], F32R) for i in range(2)]
        wa_v = [sb(f"wa_v{i}", [P, KT, D], F32R) for i in range(2)]
        wa_o = [sb(f"wa_o{i}", [P, GROUPS, D], F32R) for i in range(2)]
        wb_qk = [sb(f"wb_qk{i}", [P, KT, 2 * D], F32R) for i in range(2)]
        wb_sw = [sb(f"wb_sw{i}", [P, KT, 2 * D], F32R) for i in range(2)]
        wb_v = [sb(f"wb_v{i}", [P, KT, D], F32R) for i in range(2)]
        wb_o = [sb(f"wb_o{i}", [P, GROUPS, D], F32R) for i in range(2)]
        w_g = sb("w_g", [P, KT, HID], F32R)
        w_u = sb("w_u", [P, KT, HID], F32R)
        w_d = sb("w_d", [P, FT, D], F32R)
        cos = sb("cos", [P, S], F32)
        sin = sb("sin", [P, S], F32)
        mask0 = sb("mask0", [P, S], BF16)
        mask1 = sb("mask1", [P, 2 * WIDE[1]], BF16)
        mask3 = sb("mask3", [P, 2 * WIDE[3]], BF16)
        causal = sb("causal", [P, P], BF16)
        eye = sb("eye", [P, P], F32)
        eye_bf = sb("eye_bf", [P, P], BF16)
        sel = sb("sel", [2 * HEADS, HEADS], BF16)
        sums_sel = sb("sums_sel", [P, GROUPS], F32)
        qk_bias = sb("qk_bias", [P, 4], F32)
        v_bias = sb("v_bias", [P, D], F32)
        o_bias = [sb(f"o_bias{i}", [P, D], F32) for i in range(2)]
        eps = sb("eps", [P, NT], F32)
        pause = sb("pause", [1, 1], F32)
        minus_half = sb("minus_half", [P, NT], F32)
        w_top = sb("w_top", [P, 1], F32)
        w_top1 = sb("w_top1", [1, 1], F32)
        general = sb("general", [1, 1], I32)
        x = [sb(f"x{i}", [P, NT, D], F32) for i in range(2)]
        xn = sb("xn", [P, NT, D], F32)
        xT = [sb(f"xT{i}", [P, KT, S], F32R) for i in range(2)]
        stats = sb("stats", [P, NT, 6], F32)
        mv = sb("mv", [P, NT, 2], F32)
        veps = sb("veps", [P, NT], F32)
        root = sb("root", [P, NT], F32)
        newton = sb("newton", [P, NT], F32)
        src = sb("src", [P, 2, 2, 2, 2, S], F16)
        pack = sb("pack", [P, 2, PACK], F16)
        v_aug = [sb(f"v_aug{i}", [P, NT, HEADS, DH + 1], F32) for i in range(2)]
        top = sb("top", [P, NT, HEADS], F32)
        ntop = sb("ntop", [P, NT, 2 * HEADS], BF16)
        ntopT = sb("ntopT", [2 * HEADS, S], BF16)
        probs = sb("probs", [P, 3, S], F32)
        junk = sb("junk", [P, 3, S], BF16)
        den = [sb(f"den{i}", [P, GROUPS, NT, 4], F32) for i in range(2)]
        rden = sb("rden", [P, GROUPS, NT, 4], F32)
        o_sb = sb("o_sb", [P, GROUPS, S], F32)
        on = [sb(f"on{i}", [P, S], F32R) for i in range(2)]
        tmp = sb("tmp", [P, 2, S], F32)
        h = [sb(f"h{i}", [P, 2, S], F32R) for i in range(2)]
        s_bank = [ctx.enter_context(nc.psum_tensor(f"s_bank{i}", [P, S], F32)) for i in range(3)]
        o_bank = ctx.enter_context(nc.psum_tensor("o_bank", [P, S], F32))
        gu_bank = [ctx.enter_context(nc.psum_tensor(f"gu_bank{i}", [P, S], F32)) for i in range(2)]
        d_bank = ctx.enter_context(nc.psum_tensor("d_bank", [P, NT, D], F32))

        def q_pack(b):
            return pack[:, b, 0:PAIRS * S].rearrange("p (n s) -> p n s", s=S)

        def k_pack(b):
            return pack[:, b, PAIRS * S:PACK].rearrange("p (n s) -> p n s", s=S)

        BUFFER = {("A", 0): 1, ("A", 1): 0, ("U", 0): 1, ("U", 1): 1, ("R", 0): 0, ("R", 1): 0}

        w_in = sem("w_in")
        c_in = sem("c_in")
        zeroed = sem("zeroed")
        w_f32 = sem("w_f32")
        w_turned = sem("w_turned")
        w_taken = sem("w_taken")
        w_raw = sem("w_raw")
        w_flag = sem("w_flag")
        prep = sem("prep")
        packed = {(k, i, j): sem(f"packed_{k}{i}{j}") for k in "AUR" for i in range(2) for j in range(GROUPS)}
        a1_scores = sem("a1_scores")
        a1_taken = sem("a1_taken")
        ntop_ready = sem("ntop_ready")
        ntop_turned = sem("ntop_turned")
        ntopT_ready = sem("ntopT_ready")
        top_link = sem("top_link")
        a_scores = sem("a_scores")
        a_exp = sem("a_exp")
        a_used = sem("a_used")
        a_out_taken = sem("a_out_taken")
        den_scores = sem("den_scores")
        den_exp = sem("den_exp")
        b_scores = sem("b_scores")
        b_exp = sem("b_exp")
        b_used = sem("b_used")
        b_out_taken = sem("b_out_taken")
        x_in_sem = [sem(f"x_in{i}") for i in range(2)]
        x_stored = [sem(f"x_stored{i}") for i in range(2)]
        gu_ready = sem("gu_ready")
        gu_taken = sem("gu_taken")
        d_ready = sem("d_ready")
        d_taken = sem("d_taken")
        link = sem("link")
        mv_ready = sem("mv_ready")
        pool_link = sem("pool_link")
        root_ready = sem("root_ready")
        xn_ready = sem("xn_ready")
        xT_high = sem("xT_high")
        biased = sem("biased")
        spread_ready = sem("spread_ready")
        on_ready = sem("on_ready")
        on_used = sem("on_used")
        tanh_ready = sem("tanh_ready")
        h_high = sem("h_high")
        h_ready = sem("h_ready")
        h_used = sem("h_used")
        qk_high = sem("qk_high")
        rot_sum = sem("rot_sum")
        rot_high = sem("rot_high")
        rot_ready = sem("rot_ready")

        st = pack[:, :, :].rearrange("p b n -> p (b n)").bitcast(F32)
        at = [0]

        def stage(*shape):
            n = int(np.prod(shape))
            a = st[:, at[0]:at[0] + n]
            at[0] += n
            names = "abc"[:len(shape)]
            return a.rearrange(f"p ({' '.join(names)}) -> p {' '.join(names)}", **dict(zip(names, shape)))

        st_qkv = [stage(KT, D) for _ in range(3)]
        st_o = stage(KT, D)
        st_ocols = stage(KT, GROUPS * P)
        st_bqkv = stage(KT, 3 * D)
        st_brows = stage(GROUPS, D)
        st_int = st[:, at[0]:at[0] + 3 * FT * D].bitcast(I32)
        st_f32 = stage(3 * FT * D)
        st_dT = stage(FT, D)
        st2 = src[:, :, :, :, :, :].rearrange("p a b c d s -> p (a b c d s)").bitcast(F32)
        st_gT = st2[:, 0:KT * HID].rearrange("p (k n) -> p k n", k=KT)
        st_uT = st2[:, KT * HID:2 * KT * HID].rearrange("p (k n) -> p k n", k=KT)
        all_banks = [b[:, :] for b in s_bank] + [o_bank[:, :]] + [b[:, :] for b in gu_bank] + \
                    [d_bank[:, 0:2, :].rearrange("p a b -> p (a b)"), d_bank[:, 2:4, :].rearrange("p a b -> p (a b)")]
        NW, NC = 12, 15

        block = ctx.enter_context(nc.Block())

        @block.sync
        def _(sp):
            for st_w, w in zip(st_qkv + [st_o], (Wq, Wk, Wv, Wo)):
                sp.dma_start(st_w, w.rearrange("(t p) n -> p t n", p=P)).then_inc(w_in, 16)
            sp.dma_start(st_bqkv, Wqkv.rearrange("(t p) n -> p t n", p=P)).then_inc(w_in, 16)
            for n, w in enumerate((w_gate, w_up, w_down)):
                rows = w.shape[0] // P
                dst = st_int[:, n * FT * D:(n + 1) * FT * D].rearrange("p (t n) -> p t n", t=rows)
                sp.dma_start(dst, w.rearrange("(t p) n -> p t n", p=P)).then_inc(w_in, 16)
            sp.wait_ge(zeroed, 2)
            for c in range(4):
                rows = Wout.rearrange("(t j r d) n -> t r d j n", t=2, j=GROUPS, r=2)[c // 2, c % 2]
                sp.dma_start(st_brows[32 * c:32 * c + DH], rows).then_inc(w_in, 16)
            for dst, a in ((cos, cos_in), (sin, sin_in), (eye, eye_in), (sums_sel, sums_in)):
                sp.dma_start(dst[:, :], a).then_inc(c_in, 16)
            col = 0
            for m in (mask0, mask1, mask3, causal, eye_bf):
                n = m.shape[1]
                sp.dma_start(m[:, :], masks_in[:, col:col + n].bitcast(BF16)).then_inc(c_in, 16)
                col += n
            sp.dma_start(sel[:, :], sel_in.bitcast(BF16)).then_inc(c_in, 16)
            for n, b in enumerate((bq, bk)):
                sp.dma_start(qk_bias[:, 2 * n:2 * n + 2], b.rearrange("(t p) -> p t", p=P),
                             allow_slow_non_contiguous=True).then_inc(c_in, 16)
            for dst, b in ((v_bias, bv), (o_bias[0], bo), (o_bias[1], bout)):
                sp.dma_start(dst[:, :], b.partition_broadcast(P)).then_inc(c_in, 16)
            for i in range(2):
                sp.dma_start(x[i][:, :, :], x_in[i].rearrange("(t p) n -> p t n", p=P)).then_inc(x_in_sem[i], 16)
            for n, (dst, a) in enumerate(((w_g, st_gT), (w_u, st_uT), (w_d, st_dT))):
                sp.wait_ge(w_taken, (9, 13, 16)[n])
                sp.dma_start(dst[:, :, :].bitcast(F32), a).then_inc(w_raw, 16)

            def load_pack(kind, parity):
                b, rotated = BUFFER[kind, parity], int(kind == "R")
                qp, kp = q_pack(b), k_pack(b)
                for j in range(GROUPS):
                    for n in range(4):
                        r = slice(32 * j, 32 * j + 32)
                        sp.dma_start(qp[32 * n:32 * n + 32, 2 * j:2 * j + 2, :], src[r, rotated, 0, n // 2, :, :])\
                            .then_inc(packed[kind, parity, j], 16)
                        for e in range(2):
                            r = slice(32 * j + DH * e, 32 * j + DH * e + DH)
                            sp.dma_start(kp[32 * n + DH * e:32 * n + DH * e + DH, 4 * j + e:4 * j + e + 3:2, :],
                                         src[r, rotated, 1, n % 2, :, :]).then_inc(packed[kind, parity, j], 16)

            def slot(s, turn):
                if s.att and s.att[0] == "B":
                    _, seq, parity, _ = s.att
                    sp.wait_ge(rot_ready, (seq * 4 + 4).at(turn))
                    if parity == 0:
                        sp.wait_ge(a_scores, ((seq + 2) * A_UNITS).at(turn))
                    else:
                        sp.wait_ge(b_scores, (seq * B_UNITS).at(turn))
                    load_pack("R", parity)
                if s.out and s.out.name == "OB":
                    seq, parity = s.ffn.seq, s.ffn.parity
                    sp.wait_ge(d_taken, (s.ffn.d + 1).at(turn))
                    sp.dma_start(out[bass.ds(seq.at(turn), 1)].rearrange("a (t p) n -> p (a t) n", p=P),
                                 x[parity][:, :, :]).then_inc(x_stored[parity], 16)
                    if s.proj:
                        sp.wait_ge(x_stored[parity], Count(16, 16).at(turn))
                        sp.dma_start(x[parity][:, :, :],
                                     x_in[bass.ds((seq + 2).at(turn), 1)].rearrange("a (t p) n -> p (a t) n", p=P))\
                            .then_inc(x_in_sem[parity], 16)
                if s.proj:
                    name, seq, parity = s.proj.name, s.proj.seq, s.proj.parity
                    sp.wait_ge(gu_taken, (s.proj.gu + GU[name]).at(turn))
                    if name == "PB" and parity == 0:
                        sp.wait_ge(a_scores, ((seq + 1) * A_UNITS).at(turn))
                    elif name == "PB":
                        sp.wait_ge(den_scores, (seq * DEN_UNITS).at(turn))
                    elif parity == 0 and seq.per:
                        sp.wait_ge(den_scores, (seq * DEN_UNITS).at(turn))
                    elif seq.per:
                        sp.wait_ge(b_scores, ((seq + -1) * B_UNITS).at(turn))
                    else:
                        sp.wait_ge(zeroed, 3)
                    load_pack("U" if name == "PB" else "A", parity)

            for s in first:
                slot(s, 0)
            with sp.Fori(0, SEQS // 2 - 1) as turn:
                for s in body:
                    slot(s, turn)
            for s in tail:
                slot(s, SEQS // 2 - 1)
            for i in range(2):
                sp.wait_ge(x_stored[i], 16 * SEQS // 2)

        @block.tensor
        def _(pe):
            banks = []
            for n in range(3):
                banks.append([(k * D + t * P, st_qkv[n][:, t, k * P:(k + 1) * P]) for k in range(KT) for t in range(KT)])
            for half in range(2):
                banks.append([(j * D + t * P, st_ocols[:, t, (2 * half + j) * P:(2 * half + j + 1) * P])
                              for j in range(2) for t in range(KT)])
            for n in range(2):
                w = st_f32[:, n * FT * D:(n + 1) * FT * D].rearrange("p (t n) -> p t n", t=FT)
                for k in range(KT):
                    for half in range(2):
                        banks.append([(t * P, w[:, 3 * half + t, k * P:(k + 1) * P]) for t in range(3)])
            w = st_f32[:, 2 * FT * D:].rearrange("p (t n) -> p t n", t=KT)
            for pair in range(FT // 2):
                banks.append([(f * D + t * P, w[:, t, (2 * pair + f) * P:(2 * pair + f + 1) * P])
                              for f in range(2) for t in range(KT)])
            pe.wait_ge(c_in, 16 * NC)
            pe.wait_ge(w_in, 16 * NW)
            pe.wait_ge(w_f32, 2)
            for n, bank in enumerate(banks):
                if n >= len(all_banks):
                    pe.wait_ge(w_taken, n - len(all_banks) + 1)
                for c0, a in bank:
                    last = pe.transpose(all_banks[n % len(all_banks)][:, c0:c0 + P], a, eye[:, :])
                last.then_inc(w_turned, 1)
            pe.wait_ge(w_taken, len(banks))
            pe.wait_ge(w_flag, 1)
            pe.transpose(gu_bank[0][0:1, 0:P], w_top[:, :], eye[:, :]).then_inc(w_turned, 1)
            pe.wait_ge(w_flag, 3)
            pe.wait_ge(w_raw, 48)
            pe.wait_ge(zeroed, 3)
            is_general = pe.value_load(general[0:1, 0:1], min_val=0, max_val=1)

            def unit_bank(u):
                return s_bank[u % 3]

            def split_passes(lhs, rhs):
                return ((lhs[0], rhs[0]), (lhs[1], rhs[0]), (lhs[0], rhs[1]))

            def a_pair(s, turn, pair, by_key):
                _, seq, parity, prev = s.att
                qp, kp = q_pack(BUFFER["A", parity]), k_pack(BUFFER["A", parity])
                scores, done = (a_scores, a_exp) if by_key else (a1_scores, a1_taken)
                if not by_key and pair % 2 == 0:
                    per_turn = seq.per // 2
                    pe.wait_ge(packed["A", parity, pair // 2],
                               Count(SETDMA * (seq.const // 2 + 1), SETDMA * per_turn).at(turn))
                if pair == 0 and not by_key and prev:
                    kind, pseq = prev
                    pe.wait_ge(a_exp if kind == "A" else b_exp, ((pseq + 1) * A_UNITS).at(turn))
                if pair == 0 and by_key:
                    pe.wait_ge(ntopT_ready, (seq + 1).at(turn))
                for n, unit in enumerate(UNITS_A):
                    u = pair * NU + n
                    if u >= 3:
                        pe.wait_ge(done, (seq * A_UNITS + (u - 2)).at(turn))
                    bank = unit_bank(u)
                    mask = (mask0, mask0, mask1, mask1, mask3)[n]
                    pe.matmul(bank[:, 0:mask.shape[1]], eye_bf[:, :], mask[:, :], start=True, stop=False,
                              skip_group_check=True)
                    for e, t, c0 in unit:
                        hh = 2 * pair + e
                        stat = (kp[:, hh, :] if by_key else qp[:, pair, :])[:, t * P:(t + 1) * P]
                        moving = qp[:, pair, :] if by_key else kp[:, hh, :]
                        a, b = WINDOW[t]
                        pieces = [(c0, a, b)] + ([(c0 + b - a, 0, GLOBALS)] if t else [])
                        for c, a, b in pieces:
                            last = pe.matmul(bank[:, c:c + b - a], stat, moving[:, a:b], start=False, stop=not by_key,
                                             skip_group_check=True)
                            if by_key:
                                last = pe.matmul(bank[:, c:c + b - a], spread(sel[:, hh], P), ntopT[:, a:b],
                                                 start=False, stop=True, skip_group_check=True)
                    last.then_inc(scores, 1)
                    if by_key and u >= 2:
                        a_values(s, turn, u - 2)

            def a_values(s, turn, u):
                _, seq, parity, prev = s.att
                pair, unit = u // NU, UNITS_A[u % NU]
                if u == 0 and prev:
                    kind, pseq = prev
                    pe.wait_ge(a_out_taken if kind == "A" else b_out_taken, ((pseq + 1) * GROUPS).at(turn))
                elif u and u % (2 * NU) == 0:
                    pe.wait_ge(a_out_taken, (seq * GROUPS + u // (2 * NU)).at(turn))
                pe.wait_ge(a_exp, (seq * A_UNITS + (u + 1)).at(turn))
                for e, t, c0 in unit:
                    hh = 2 * pair + e
                    strip = 2 * (pair % 2) + e
                    v = v_aug[parity][:, t, 8 * (pair % 2) + 2 * (pair // 2) + e, :]
                    a, b = WINDOW[t]
                    for c, a, b in [(c0, a, b)] + ([(c0 + b - a, 0, GLOBALS)] if t else []):
                        last = pe.matmul(o_bank[32 * strip:32 * strip + DH + 1, a:b], v, probs[:, u % 3, c:c + b - a],
                                         start=t == 0, stop=t == NT - 1, tile_position=(0, 32 * strip),
                                         skip_group_check=True)
                last.then_inc(a_used, 1)

            def turn_maxima(s, turn):
                _, seq, parity, _ = s.att
                pe.wait_ge(ntop_ready, (seq + 1).at(turn))
                for t in range(NT):
                    last = pe.matmul(unit_bank(0)[0:2 * HEADS, t * P:(t + 1) * P], ntop[:, t, :], eye_bf[:, :],
                                     start=True, stop=True)
                last.then_inc(ntop_turned, 1)

            def den_pair(s, turn, pair):
                _, seq, parity, prev = s.att
                qp, kp = q_pack(BUFFER["U", parity]), k_pack(BUFFER["U", parity])
                if pair % 2 == 0:
                    pe.wait_ge(packed["U", parity, pair // 2], Count(SETDMA, SETDMA).at(turn))
                if pair == 0:
                    kind, pseq = prev
                    pe.wait_ge(a_exp if kind == "A" else b_exp, ((pseq + 1) * A_UNITS).at(turn))
                for e in range(2):
                    for t in range(NT):
                        u = (2 * pair + e) * NT + t
                        if u >= 3:
                            pe.wait_ge(den_exp, (seq * DEN_UNITS + (u - 2)).at(turn))
                        pe.matmul(unit_bank(u)[:, :], qp[:, pair, t * P:(t + 1) * P], kp[:, 2 * pair + e, :],
                                  start=True, stop=True).then_inc(den_scores, 1)

            def b_pair(s, turn, pair):
                _, seq, parity, _ = s.att
                qp, kp = q_pack(BUFFER["R", parity]), k_pack(BUFFER["R", parity])
                if pair % 2 == 0:
                    pe.wait_ge(packed["R", parity, pair // 2], Count(SETDMA, SETDMA).at(turn))
                if pair == 0:
                    pe.wait_ge(den_exp, ((seq + 1) * DEN_UNITS).at(turn))
                for n, unit in enumerate(UNITS_B):
                    u = pair * NU + n
                    if u >= 3:
                        pe.wait_ge(b_exp, (seq * B_UNITS + (u - 2)).at(turn))
                    bank = unit_bank(u)
                    for i, (e, t, c0) in enumerate(unit):
                        pe.matmul(bank[:, c0:c0 + P], eye_bf[:, :], causal[:, :], start=i == 0, stop=False,
                                  skip_group_check=True)
                    for e, t, c0 in unit:
                        last = pe.matmul(bank[:, c0:c0 + S - t * P], kp[:, 2 * pair + e, t * P:(t + 1) * P],
                                         qp[:, pair, t * P:S], start=False, stop=True, skip_group_check=True)
                    last.then_inc(b_scores, 1)
                    if u >= 2:
                        b_values(s, turn, u - 2)

            def b_values(s, turn, u):
                _, seq, parity, prev = s.att
                pair, unit = u // NU, UNITS_B[u % NU]
                if u % (2 * NU) == 0:
                    if u == 0:
                        kind, pseq = prev
                        pe.wait_ge(a_out_taken if kind == "A" else b_out_taken, ((pseq + 1) * GROUPS).at(turn))
                    else:
                        pe.wait_ge(b_out_taken, (seq * GROUPS + u // (2 * NU)).at(turn))
                pe.wait_ge(b_exp, (seq * B_UNITS + (u + 1)).at(turn))
                for e, t, c0 in unit:
                    strip = 2 * (pair % 2) + e
                    v = v_aug[parity][:, t, 8 * (pair % 2) + 2 * (pair // 2) + e, 0:DH]
                    last = pe.matmul(o_bank[32 * strip:32 * strip + DH, t * P:S], v, probs[:, u % 3, c0:c0 + S - t * P],
                                     start=t == 0, stop=t == NT - 1, tile_position=(0, 32 * strip),
                                     skip_group_check=True)
                last.then_inc(b_used, 1)

            def gu(block, k, turn):
                if (block.gu + (k - 1)).const > 0:
                    pe.wait_ge(gu_taken, (block.gu + (k - 1)).at(turn))
                return gu_bank[k % 2]

            def out_step(block, n, turn):
                w = wa_o if block.name == "OA" else wb_o
                if n == 0:
                    pe.wait_ge(d_taken, block.d.at(turn))
                    if block.name == "OA":
                        pe.wait_ge(a_out_taken, ((block.seq + 1) * GROUPS).at(turn))
                        for j in range(GROUPS):
                            for t in range(NT):
                                k = (j * NT + t) * 4
                                last = pe.matmul(d_bank[:, 0, k:k + 4], o_sb[:, j, t * P:(t + 1) * P], sums_sel[:, :],
                                                 start=True, stop=True)
                        last.then_inc(d_ready, 1)
                if n < GROUPS:
                    bank = gu(block, n, turn)
                    pe.wait_ge(spread_ready, (block.o * GROUPS + (n + 1)).at(turn))
                    for t in range(NT):
                        last = pe.transpose(bank[:, t * P:(t + 1) * P], tmp[:, n % 2, t * P:(t + 1) * P], eye[:, :])
                    last.then_inc(gu_ready, 1)
                if n >= 1:
                    j = n - 1
                    if n == 1 and block.name == "OA":
                        pe.wait_ge(d_taken, (block.d + 1).at(turn))
                    pe.wait_ge(on_ready, (block.o * GROUPS + n).at(turn))
                    for t in range(NT):
                        for i, (a, b) in enumerate(split_passes(on, w)):
                            last = pe.matmul(d_bank[:, t, :], a[:, t * P:(t + 1) * P], b[:, j, :],
                                             start=j == 0 and i == 0 and t % 2 == 0, stop=j == GROUPS - 1 and i == 2,
                                             skip_group_check=True)
                    last.then_inc(d_ready if n == GROUPS else on_used, 1)

            def turn_x(block, turn):
                pe.wait_ge(xn_ready, (block.ln + 1).at(turn))
                for k in range(KT):
                    bank = gu(block, k, turn)
                    for t in range(NT):
                        last = pe.transpose(bank[:, t * P:(t + 1) * P], xn[:, t, k * P:(k + 1) * P], eye[:, :])
                    last.then_inc(gu_ready, 1)

            def plain(a, exact):
                return a if exact else a.bitcast(F32)

            def ffn_up(block, f, turn, exact):
                for n, w in enumerate((w_g, w_u)):
                    bank = gu_bank[n]
                    for k in range(KT):
                        for i in range(2):
                            last = pe.matmul(bank[:, :], plain(w[:, k, f * P:(f + 1) * P], exact), plain(xT[i][:, k, :], exact),
                                             start=k == 0 and i == 0, stop=k == KT - 1 and i == 1)
                    last.then_inc(gu_ready, 1)

            def ffn_down(block, f, turn, exact):
                for t in range(NT):
                    for i in range(2):
                        last = pe.matmul(d_bank[:, t, :], plain(h[i][:, f % 2, t * P:(t + 1) * P], exact),
                                         plain(w_d[:, f, :], exact), start=f == 0 and i == 0 and t % 2 == 0,
                                         stop=f == FT - 1 and i == 1, skip_group_check=True)
                last.then_inc(d_ready if f == FT - 1 else h_used, 1)

            def ffn_step(block, n, turn):
                if n < FT:
                    pe.wait_ge(gu_taken, (block.gu + (KT + 2 * n)).at(turn))
                    with pe.If(is_general > 0):
                        ffn_up(block, n, turn, False)
                    with pe.Else():
                        ffn_up(block, n, turn, True)
                if n >= 1:
                    if n == 1:
                        pe.wait_ge(d_taken, block.d.at(turn))
                    pe.wait_ge(h_ready, (block.f * FT + n).at(turn))
                    with pe.If(is_general > 0):
                        ffn_down(block, n - 1, turn, False)
                    with pe.Else():
                        ffn_down(block, n - 1, turn, True)

            def qk_step(block, n, turn):
                if n == 0:
                    pe.wait_ge(gu_taken, (block.gu + KT).at(turn))
                pa = block.name == "PA"
                for m, w in enumerate((wa_qk,) if pa else (wb_qk, wb_sw)):
                    bank = gu(block, KT + (n if pa else 2 * n + m), turn)
                    for k in range(KT):
                        for i, (a, b) in enumerate(split_passes(w, xT)):
                            last = pe.matmul(bank[:, :], a[:, k, n * P:(n + 1) * P], b[:, k, :],
                                             start=k == 0 and i == 0, stop=k == KT - 1 and i == 2)
                    last.then_inc(gu_ready, 1)

            def v_step(block, turn):
                w = wa_v if block.name == "PA" else wb_v
                if block.d.const:
                    pe.wait_ge(d_taken, block.d.at(turn))
                for t in range(NT):
                    for k in range(KT):
                        for i, (a, b) in enumerate(split_passes(xT, w)):
                            last = pe.matmul(d_bank[:, t, :], a[:, k, t * P:(t + 1) * P], b[:, k, :],
                                             start=k == 0 and i == 0 and t % 2 == 0, stop=k == KT - 1 and i == 2,
                                             skip_group_check=True)
                last.then_inc(d_ready, 1)

            def slot(s, turn):
                for tick in range(2 * PAIRS):
                    pair, second = tick % PAIRS, tick >= PAIRS
                    if s.att and s.att[0] == "A":
                        if tick == PAIRS:
                            turn_maxima(s, turn)
                        a_pair(s, turn, pair, second)
                    elif s.att:
                        (b_pair if second else den_pair)(s, turn, pair)
                    if s.att and tick == 2 * PAIRS - 1:
                        for u in (A_UNITS - 2, A_UNITS - 1):
                            (a_values if s.att[0] == "A" else b_values)(s, turn, u)
                    for kind, n, block in s.steps(tick):
                        if kind == "O":
                            out_step(block, n, turn)
                        elif kind == "LN":
                            turn_x(block, turn)
                        elif kind == "F":
                            ffn_step(block, n, turn)
                        elif kind == "T":
                            qk_step(block, n, turn)
                        else:
                            v_step(block, turn)

            for s in first:
                slot(s, 0)
            with pe.Fori(0, SEQS // 2 - 1) as turn:
                for s in body:
                    slot(s, turn)
            for s in tail:
                slot(s, SEQS // 2 - 1)

        @block.scalar
        def _(act):
            def prev_used(s, turn):
                kind, pseq = s.att[3]
                act.wait_ge(a_used if kind == "A" else b_used, ((pseq + 1) * A_UNITS).at(turn))

            def exps(s, turn, pair, scores, done, used, units, widths):
                _, seq, parity, prev = s.att
                if pair == 0 and prev:
                    prev_used(s, turn)
                for n in range(NU):
                    u = pair * NU + n
                    act.wait_ge(scores, (seq * A_UNITS + (u + 1)).at(turn))
                    if u >= 3:
                        act.wait_ge(used, (seq * A_UNITS + (u - 2)).at(turn))
                    act.activation(probs[:, u % 3, 0:widths[n]], s_bank[u % 3][:, 0:widths[n]], ACT.Exp,
                                   scale=SM_SCALE).then_inc(done, 1)

            def den_exps(s, turn, pair):
                _, seq, parity, _ = s.att
                for e in range(2):
                    for t in range(NT):
                        u = (2 * pair + e) * NT + t
                        act.wait_ge(den_scores, (seq * DEN_UNITS + (u + 1)).at(turn))
                        act.activation(junk[:, u % 3, :], s_bank[u % 3][:, :], ACT.Exp, scale=SM_SCALE,
                                       accum_out=den[parity][:, pair // 2, t, 2 * (pair % 2) + e:2 * (pair % 2) + e + 1])\
                            .then_inc(den_exp, 1)

            def x_high(block, turn):
                for k in range(KT):
                    act.wait_ge(gu_ready, (block.gu + (k + 1)).at(turn))
                    act.activation(xT[0][:, k, :], gu_bank[k % 2][:, :], ACT.Copy).then_inc(xT_high, 1)

            def ffn_step(block, f, turn):
                if f >= 2:
                    act.wait_ge(h_ready, (block.f * FT + (f - 1)).at(turn))
                act.wait_ge(gu_ready, (block.gu + (KT + 2 * f + 1)).at(turn))
                act.activation(tmp[:, f % 2, :], gu_bank[0][:, :], ACT.Tanh, scale=0.5 * DEQUANT).then_inc(tanh_ready, 1)

            def qk_step(block, n, att, turn):
                pa = block.name == "PA"
                k = KT + (n if pa else 2 * n)
                act.wait_ge(gu_ready, (block.gu + (k + 1)).at(turn))
                dst = src[:, 0, n // 2, 0, n % 2, :]
                if pa:
                    act.activation(dst, gu_bank[k % 2][:, :], ACT.Identity, bias=qk_bias[:, n:n + 1]).then_inc(qk_high, 1)
                else:
                    act.activation(dst, gu_bank[k % 2][:, :], ACT.Copy).then_inc(qk_high, 1)
                    act.wait_ge(rot_sum, (block.seq * 4 + (n + 1)).at(turn))
                    if n == 0 and att[0] == "B":
                        for j in range(GROUPS):
                            act.wait_ge(packed["R", att[2], j], Count(SETDMA, SETDMA).at(turn))
                    act.activation(src[:, 1, n // 2, 0, n % 2, :], tmp[:, 0, :], ACT.Copy).then_inc(rot_high, 1)

            def slot(s, turn):
                for tick in range(2 * PAIRS):
                    pair, second = tick % PAIRS, tick >= PAIRS
                    if s.att and s.att[0] == "A" and second:
                        if tick == PAIRS:
                            act.wait_ge(ntop_turned, (s.att[1] + 1).at(turn))
                            act.activation(ntopT[:, :], s_bank[0][0:2 * HEADS, :], ACT.Copy).then_inc(ntopT_ready, 1)
                        exps(s, turn, pair, a_scores, a_exp, a_used, UNITS_A, (S, S, 2 * WIDE[1], 2 * WIDE[1], 2 * WIDE[3]))
                    elif s.att and s.att[0] == "B" and second:
                        exps(s, turn, pair, b_scores, b_exp, b_used, UNITS_B, (S,) * NU)
                    elif s.att and s.att[0] == "B":
                        den_exps(s, turn, pair)
                    for kind, n, block in s.steps(tick):
                        if kind == "LN":
                            x_high(block, turn)
                        elif kind == "F" and n < FT:
                            ffn_step(block, n, turn)
                        elif kind == "T":
                            qk_step(block, n, s.att, turn)

            act.wait_ge(c_in, 16 * NC)
            act.wait_ge(w_raw, 48)
            for s in first:
                slot(s, 0)
            with act.Fori(0, SEQS // 2 - 1) as turn:
                for s in body:
                    slot(s, turn)
            for s in tail:
                slot(s, SEQS // 2 - 1)

        @block.vector
        def _(dve):
            done = [0]

            def then(ins):
                done[0] += 1
                ins.then_inc(prep, 1)
                dve.wait_ge(prep, done[0])

            def split(parts, a):
                then(dve.tensor_copy(parts[0], a))
                return dve.tensor_tensor(parts[1], a, parts[0].bitcast(F32), ALU.subtract)

            dve.memset(st_ocols, 0.0).then_inc(zeroed, 1)
            dve.memset(st_brows, 0.0).then_inc(zeroed, 1)
            dve.wait_ge(zeroed, 2)
            dve.wait_ge(w_in, 16 * NW)
            for t in range(KT):
                for c in range(2):
                    dst = st_ocols[:, t, :].rearrange("p (j a r d) -> p j a r d", j=GROUPS, a=2, r=2)[:, :, c, :, 0:DH]
                    a = st_o[:, t, :].rearrange("p (a j r d) -> p a j r d", a=2, j=GROUPS, r=2)[:, c, :, :, :]
                    last = dve.tensor_copy(dst, a)
            last.then_inc(w_f32, 1)
            dve.tensor_copy(st_f32, st_int).then_inc(w_f32, 1)
            dve.wait_ge(w_f32, 2)
            dve.tensor_reduce(w_top[:, :], st_f32, axis=AX.X, op=ALU.max, apply_absolute_value=True).then_inc(w_flag, 1)
            split([w[:, :, :] for w in wb_qk], st_bqkv[:, :, 0:2 * D])
            split([w[:, :, :] for w in wb_v], st_bqkv[:, :, 2 * D:3 * D])
            for e in range(2):
                split([w[:, :, 1 - e::2] for w in wb_sw], st_bqkv[:, :, e:2 * D:2])
            split([w[:, :, :] for w in wb_o], st_brows)
            for n in range(16):
                dve.wait_ge(w_turned, n + 1)
                bank = all_banks[n % len(all_banks)]
                if n < 3:
                    w, c = ((wa_qk, 0), (wa_qk, D), (wa_v, 0))[n]
                    split([a[:, :, c:c + D] for a in w], bank.rearrange("p (k n) -> p k n", k=KT)).then_inc(w_taken, 1)
                elif n < 5:
                    j = 2 * (n - 3)
                    split([a[:, j:j + 2, :] for a in wa_o], bank.rearrange("p (k n) -> p k n", k=2)).then_inc(w_taken, 1)
                elif n < 13:
                    dst, k, half = (st_gT, st_uT)[(n - 5) // 4], (n - 5) // 2 % 2, (n - 5) % 2
                    dve.tensor_copy(dst[:, k, half * 3 * P:(half + 1) * 3 * P], bank[:, 0:3 * P]).then_inc(w_taken, 1)
                else:
                    f = 2 * (n - 13)
                    dve.tensor_copy(st_dT[:, f:f + 2, :], bank.rearrange("p (k n) -> p k n", k=2)).then_inc(w_taken, 1)
            dve.wait_ge(w_turned, 17)
            dve.tensor_reduce(w_top1[:, :], gu_bank[0][0:1, 0:P], axis=AX.X, op=ALU.max).then_inc(w_flag, 1)
            dve.wait_ge(w_flag, 2)
            dve.tensor_single_scalar(general[:, :], w_top1[:, :], EXACT, ALU.is_gt).then_inc(w_flag, 1)
            dve.memset(o_bank[:, :], 0.0)
            for i in range(2):
                dve.memset(v_aug[i][:, :, :, :], 1.0)
            dve.wait_ge(w_raw, 48)
            dve.memset(pack[:, :, :].rearrange("p b n -> p (b n)").bitcast(F32), 0.0).then_inc(zeroed, 1)
            dve.wait_ge(zeroed, 3)

            def a_maxima(s, turn, pair):
                _, seq, parity, _ = s.att
                for n, unit in enumerate(UNITS_A):
                    u, hh = pair * NU + n, 2 * pair
                    dve.wait_ge(a1_scores, (seq * A_UNITS + (u + 1)).at(turn))
                    bank = s_bank[u % 3]
                    if n < 2:
                        dst, a = top[:, 0, hh + n:hh + n + 1], bank[:, :]
                    elif n < 4:
                        dst = top[:, 1:3, hh + n - 2]
                        a = bank[:, 0:2 * WIDE[1]].rearrange("p (a b) -> p a b", a=2)
                    else:
                        dst = top[:, 3, hh:hh + 2]
                        a = bank[:, 0:2 * WIDE[3]].rearrange("p (a b) -> p a b", a=2)
                    dve.reduce_max(dst, a, AX.X).then_inc(a1_taken, 1)

            def minus_maxima(s, turn):
                _, seq, parity, _ = s.att
                dve.wait_ge(a1_taken, ((seq + 1) * A_UNITS).at(turn))
                dve.tensor_scalar(ntop[:, :, 0:HEADS], top[:, :, :], -1.0, None, ALU.mult).then_inc(top_link, 1)
                dve.wait_ge(top_link, (seq + 1).at(turn))
                dve.scalar_tensor_tensor(ntop[:, :, HEADS:2 * HEADS], top[:, :, :], -1.0, ntop[:, :, 0:HEADS],
                                         ALU.mult, ALU.subtract).then_inc(ntop_ready, 1)

            def take_out(s, turn, j):
                kind, seq, parity, _ = s.att
                used, taken = (a_used, a_out_taken) if kind == "A" else (b_used, b_out_taken)
                dve.wait_ge(used, (seq * A_UNITS + (j + 1) * 2 * NU).at(turn))
                dve.tensor_copy(o_sb[:, j, :], o_bank[:, :]).then_inc(taken, 1)

            def linked(block, n, ins, turn):
                ins.then_inc(link, 1)
                dve.wait_ge(link, (block.link + n).at(turn))

            def spread_group(block, j, turn):
                dst = tmp[:, j % 2, :].rearrange("p (a b) -> p a b", b=32)
                dve.tensor_copy(dst, spread(rden[:, j, :, :].rearrange("p t c -> p (t c)"), 32)).then_inc(spread_ready, 1)

            def out_step(block, n, turn):
                if n == 0:
                    if block.pb.const:
                        dve.wait_ge(rot_ready, (block.pb * 4).at(turn))
                    if block.name == "OA":
                        dve.wait_ge(d_ready, (block.d + 1).at(turn))
                        dve.reciprocal(rden[:, :, :, :].rearrange("p j t c -> p (j t c)"), d_bank[:, 0, 0:4 * GROUPS * NT])\
                            .then_inc(d_taken, 1)
                        dve.wait_ge(d_taken, (block.d + 1).at(turn))
                    else:
                        dve.wait_ge(den_exp, ((block.seq + 1) * DEN_UNITS).at(turn))
                        linked(block, 1, dve.reciprocal(rden[:, :, :, :].rearrange("p j t c -> p (j t c)"),
                                                        den[block.parity][:, :, :, :].rearrange("p j t c -> p (j t c)")), turn)
                    spread_group(block, 0, turn)
                if n < GROUPS:
                    if n + 1 < GROUPS:
                        spread_group(block, n + 1, turn)
                    dve.wait_ge(gu_ready, (block.gu + (n + 1)).at(turn))
                    dve.tensor_tensor(o_sb[:, n, :], o_sb[:, n, :], gu_bank[n % 2][:, :], ALU.mult).then_inc(gu_taken, 1)
                    dve.wait_ge(gu_taken, (block.gu + (n + 1)).at(turn))
                    if n:
                        dve.wait_ge(on_used, (block.o * (GROUPS - 1) + n).at(turn))
                    linked(block, n + LINKS[block.name] - GROUPS + 1, dve.tensor_copy(on[0][:, :], o_sb[:, n, :]), turn)
                    dve.tensor_tensor(on[1][:, :], o_sb[:, n, :], on[0][:, :].bitcast(F32), ALU.subtract)\
                        .then_inc(on_ready, 1)
                else:
                    xs = x[block.parity][:, :, :]
                    dve.wait_ge(biased, block.p.at(turn))
                    dve.wait_ge(d_ready, (block.d + DU[block.name]).at(turn))
                    dve.tensor_tensor(xs, xs, d_bank[:, :, :], ALU.add).then_inc(d_taken, 1)
                    dve.wait_ge(d_taken, (block.d + DU[block.name]).at(turn))

            def normalise(block, turn):
                xs = x[block.parity]
                if block.name == "PA":
                    dve.wait_ge(x_in_sem[block.parity], (Count(16 * (block.seq.const // 2 + 1), 16 * (block.seq.per // 2))).at(turn))
                for t in range(NT):
                    ins = dve.bn_stats(stats[:, t, :], xs[:, t, :])
                linked(block, 1, ins, turn)
                dve.memset(pause[:, :], 0.0)
                for t in range(NT):
                    ins = dve.bn_aggr(mv[:, t, :], stats[:, t, :])
                ins.then_inc(mv_ready, 1)
                dve.wait_ge(root_ready, (block.ln + 1).at(turn))
                linked(block, 2, dve.tensor_tensor(newton[:, :], root[:, :], root[:, :], ALU.mult), turn)
                linked(block, 3, dve.tensor_tensor(newton[:, :], newton[:, :], veps[:, :], ALU.mult), turn)
                linked(block, 4, dve.tensor_scalar(newton[:, :], newton[:, :], -0.5, 1.5, ALU.mult, ALU.add), turn)
                linked(block, 5, dve.tensor_tensor(root[:, :], root[:, :], newton[:, :], ALU.mult), turn)
                for t in range(NT):
                    ins = dve.tensor_scalar(xn[:, t, :], xs[:, t, :], mv[:, t, 0:1], root[:, t:t + 1], ALU.subtract, ALU.mult)
                ins.then_inc(xn_ready, 1)
                for k in range(KT):
                    dve.wait_ge(xT_high, (block.ln * KT + (k + 1)).at(turn))
                    dve.tensor_tensor(xT[1][:, k, :], gu_bank[k % 2][:, :], xT[0][:, k, :].bitcast(F32), ALU.subtract)\
                        .then_inc(gu_taken, 1)
                    dve.wait_ge(gu_taken, (block.gu + (k + 1)).at(turn))

            def ffn_step(block, f, turn):
                if f < FT:
                    t = tmp[:, f % 2, :]
                    dve.wait_ge(tanh_ready, (block.f * FT + (f + 1)).at(turn))
                    k = block.gu + (KT + 2 * f + 1)
                    dve.scalar_tensor_tensor(t, t, 1.0, gu_bank[0][:, :], ALU.add, ALU.mult).then_inc(gu_taken, 1)
                    dve.wait_ge(gu_taken, k.at(turn))
                    dve.wait_ge(gu_ready, (k + 1).at(turn))
                    dve.tensor_tensor(t, t, gu_bank[1][:, :], ALU.mult).then_inc(gu_taken, 1)
                    dve.wait_ge(gu_taken, (k + 1).at(turn))
                    if f >= 2:
                        dve.wait_ge(h_used, (block.f * (FT - 1) + (f - 1)).at(turn))
                    dve.tensor_copy(h[0][:, f % 2, :], t).then_inc(h_high, 1)
                else:
                    xs = x[block.parity][:, :, :]
                    dve.wait_ge(d_ready, (block.d + 1).at(turn))
                    dve.scalar_tensor_tensor(xs, d_bank[:, :, :], 0.5 * DEQUANT ** 3, xs, ALU.mult, ALU.add)\
                        .then_inc(d_taken, 1)
                    dve.wait_ge(d_taken, (block.d + 1).at(turn))

            def qk_step(block, n, turn):
                pa = block.name == "PA"
                k = KT + (n if pa else 2 * n)
                dve.wait_ge(qk_high, (block.p * 4 + (n + 1)).at(turn))
                hi, lo = src[:, 0, n // 2, 0, n % 2, :], src[:, 0, n // 2, 1, n % 2, :]
                if pa:
                    dve.scalar_tensor_tensor(lo, gu_bank[k % 2][:, :], qk_bias[:, n:n + 1], hi, ALU.add, ALU.subtract)\
                        .then_inc(gu_taken, 1)
                else:
                    dve.tensor_tensor(lo, gu_bank[0][:, :], hi, ALU.subtract)
                    if n:
                        dve.wait_ge(rot_ready, (block.seq * 4 + n).at(turn))
                    dve.tensor_tensor(tmp[:, 0, :], gu_bank[0][:, :], cos[:, :], ALU.mult).then_inc(gu_taken, 1)
                    dve.wait_ge(gu_ready, (block.gu + (k + 2)).at(turn))
                    dve.tensor_tensor(tmp[:, 1, :], gu_bank[1][:, :], sin[:, :], ALU.mult).then_inc(gu_taken, 1)

            def v_step(block, turn):
                dve.wait_ge(d_ready, (block.d + 1).at(turn))
                for t in range(NT):
                    dst = v_aug[block.parity][:, t, :, 0:DH]
                    a = d_bank[:, t, :].rearrange("p (h d) -> p h d", h=HEADS)
                    if block.name == "PA":
                        ins = dve.tensor_tensor(dst, a, v_bias[:, :].rearrange("p (h d) -> p h d", h=HEADS), ALU.add)
                    else:
                        ins = dve.tensor_copy(dst, a)
                ins.then_inc(d_taken, 1)

            def slot(s, turn):
                for tick in range(2 * PAIRS):
                    pair, second = tick % PAIRS, tick >= PAIRS
                    if s.att and s.att[0] == "A" and not second:
                        a_maxima(s, turn, pair)
                        if pair == PAIRS - 1:
                            minus_maxima(s, turn)
                    if s.att and second and pair and pair % 2 == 0:
                        take_out(s, turn, pair // 2 - 1)
                    for kind, n, block in s.steps(tick):
                        if kind == "O":
                            out_step(block, n, turn)
                        elif kind == "LN":
                            normalise(block, turn)
                        elif kind == "F":
                            ffn_step(block, n, turn)
                        elif kind == "T":
                            qk_step(block, n, turn)
                        else:
                            v_step(block, turn)
                if s.att:
                    take_out(s, turn, GROUPS - 1)

            for s in first:
                slot(s, 0)
            with dve.Fori(0, SEQS // 2 - 1) as turn:
                for s in body:
                    slot(s, turn)
            for s in tail:
                slot(s, SEQS // 2 - 1)

        @block.gpsimd
        def _(pool):
            pool.memset(minus_half[:, :], -0.5).then_inc(pool_link, 1)
            pool.memset(eps[:, :], EPS).then_inc(pool_link, 1)
            pool.wait_ge(pool_link, 2)
            pool.wait_ge(c_in, 16 * NC)

            def rsqrt(block, turn):
                pool.wait_ge(mv_ready, (block.ln + 1).at(turn))
                pool.tensor_tensor(veps[:, :], mv[:, :, 1], eps[:, :], ALU.add).then_inc(pool_link, 1)
                pool.wait_ge(pool_link, (block.ln + 3).at(turn))
                pool.tensor_tensor(root[:, :], veps[:, :], minus_half[:, :], ALU.pow).then_inc(root_ready, 1)

            def add_bias(block, turn):
                pool.wait_ge(xn_ready, (block.ln + 1).at(turn))
                xs = x[block.parity]
                for t in range(NT):
                    ins = pool.tensor_tensor(xs[:, t, :], xs[:, t, :], o_bias[block.name == "PB"][:, :], ALU.add)
                ins.then_inc(biased, 1)

            def ffn_step(block, f, turn):
                pool.wait_ge(h_high, (block.f * FT + (f + 1)).at(turn))
                pool.tensor_tensor(h[1][:, f % 2, :], tmp[:, f % 2, :], h[0][:, f % 2, :].bitcast(F32), ALU.subtract)\
                    .then_inc(h_ready, 1)

            def rotate(block, n, turn):
                pool.wait_ge(gu_taken, (block.gu + (KT + 2 * n + 2)).at(turn))
                pool.tensor_tensor(tmp[:, 0, :], tmp[:, 0, :], tmp[:, 1, :], ALU.add).then_inc(rot_sum, 1)
                pool.wait_ge(rot_high, (block.seq * 4 + (n + 1)).at(turn))
                pool.tensor_tensor(src[:, 1, n // 2, 1, n % 2, :], tmp[:, 0, :], src[:, 1, n // 2, 0, n % 2, :], ALU.subtract)\
                    .then_inc(rot_ready, 1)

            def slot(s, turn):
                for tick in range(2 * PAIRS):
                    for kind, n, block in s.steps(tick):
                        if kind == "LN":
                            rsqrt(block, turn)
                            if block.name != "F":
                                add_bias(block, turn)
                        elif kind == "F" and n < FT:
                            ffn_step(block, n, turn)
                        elif kind == "T" and block.name == "PB":
                            rotate(block, n, turn)

            for s in first:
                slot(s, 0)
            with pool.Fori(0, SEQS // 2 - 1) as turn:
                for s in body:
                    slot(s, turn)
            for s in tail:
                slot(s, SEQS // 2 - 1)


def shape_constants():
    i = np.arange(DH // 2, dtype=np.float32)
    theta = np.power(np.float32(10000.0), np.float32(-2.0) * (i - np.float32(1.0)) / np.float32(DH)).astype(np.float32)
    angle = (np.arange(S, dtype=np.float32)[:, None] * theta[None, :]).astype(np.float32)
    d = np.arange(P) % DH
    cos = np.cos(angle)[:, d // 2].T
    sin = np.sin(angle)[:, d // 2].T * np.where(d % 2, 1.0, -1.0)[:, None]
    r = np.arange(P)[:, None]
    c = np.arange(S)[None, :]
    seen = (np.abs(r - c) <= HALF) | (c < GLOBALS) | (r < GLOBALS)
    masks = [np.where(seen, 0.0, MASKED)]
    for t in (1, 3):
        a, b = WINDOW[t]
        near = np.abs(r + t * P - np.arange(a, b)[None, :]) <= HALF
        near = np.concatenate([near, np.ones((P, GLOBALS), bool)], 1)
        masks.append(np.tile(np.where(near, 0.0, MASKED), (1, 2)))
    masks.append(np.where(r <= np.arange(P)[None, :], 0.0, MASKED))
    masks.append(np.eye(P))
    sel = (np.arange(2 * HEADS)[:, None] % HEADS == np.arange(HEADS)[None, :])
    sums = (np.arange(P)[:, None] == 32 * np.arange(GROUPS)[None, :] + DH)
    f = lambda a, t: np.ascontiguousarray(a, dtype=t)
    bf16 = lambda a: np.ascontiguousarray(f(a, np.float32).view(np.uint32) >> 16, dtype=np.uint16)
    return {"cos": f(cos, np.float32), "sin": f(sin, np.float32),
            "masks": bf16(np.concatenate(masks, 1)), "eye": f(np.eye(P), np.float32),
            "sel": bf16(sel), "sums": f(sums, np.float32)}


_INS = ["L0_attn_a_x", "L0_attn_a_Wq", "L0_attn_a_bq", "L0_attn_a_Wk", "L0_attn_a_bk", "L0_attn_a_Wv", "L0_attn_a_bv",
        "L0_attn_a_Wo", "L0_attn_a_bo", "L0_attn_b_Wqkv", "L0_attn_b_Wout", "L0_attn_b_bout", "L0_ffn_w_gate",
        "L0_ffn_w_up", "L0_ffn_w_down"]


def kernel(**inputs):
    import numpy as _np
    import concourse.bacc as _bacc
    from concourse import mybir as _mybir
    from concourse.bass_utils import run_bass_kernel_spmd as _run

    nc = _bacc.Bacc("TRN2", target_bir_lowering=False, num_devices=1)
    arrays, args = {}, []
    given = {n: _np.ascontiguousarray(inputs[n]) for n in _INS}
    for name, a in {**given, **shape_constants()}.items():
        arrays[f"in_{name}_dram"] = a
        args.append(nc.dram_tensor(f"in_{name}_dram", a.shape, _mybir.dt.from_np(a.dtype), kind="ExternalInput").ap())
    args.append(nc.dram_tensor("out_dram", (SEQS, S, D), _mybir.dt.float32, kind="ExternalOutput").ap())
    build(nc, *args)
    r = _run(nc, [arrays], core_ids=[0])
    return r.results[0]["out_dram"]
```

```python
import numpy as np
import concourse.bass as bass
from concourse import mybir
from concourse.alu_op_type import AluOpType as ALU
from contextlib import ExitStack

F32, F32R = mybir.dt.float32, mybir.dt.float32r
F16, BF16, I32 = mybir.dt.float16, mybir.dt.bfloat16, mybir.dt.int32
ACT = mybir.ActivationFunctionType
AX = mybir.AxisListType

SEQS, S, D = 16, 512, 256
HEADS, DH = 16, 16
HID = 768
P = 128
NT, KT, FT = S // P, D // P, HID // P
GROUPS = 4
PAIRS = HEADS // 2
PACK = HEADS // 2 * S + HEADS * S
HALF, GLOBALS = 32, 4
MASKED = -1e30
EPS = 1e-5
SM_SCALE = float(DH) ** -0.5
DEQUANT = float(np.float32(1.0 / 127.0))
EXACT = 2048.0

WINDOW = [(0, S)] + [(t * P - HALF, min((t + 1) * P + HALF, S)) for t in range(1, NT)]
WIDE = [b - a + (GLOBALS if t else 0) for t, (a, b) in enumerate(WINDOW)]
UNITS_A = [[(c, 0, 0)] for c in range(4)] + [[(c, 1, 0), (c, 2, WIDE[1])] for c in range(4)] + \
          [[(c, 3, 0), (c + 1, 3, WIDE[3])] for c in (0, 2)]
UNITS_B = [[(c, 0, 0)] for c in range(4)] + [[(c, 1, 0), (c, 3, 3 * P)] for c in range(4)] + \
          [[(c, 2, 0), (c + 1, 2, 2 * P)] for c in (0, 2)]
NU = len(UNITS_A)
BATCHES = [(0, 1, 2, 3), (4, 5, 6, 7), (8, 9)]
BATCH_OF = [b for b, units in enumerate(BATCHES) for _ in units]
LAG = 2
RING = 6
UNITS = GROUPS * NU
USES = GROUPS * len(BATCHES)
DEN_UNITS = HEADS * NT
SETDMA = 12 * 16
GU = {"OA": GROUPS, "OB": GROUPS, "F": KT + 2 * FT, "PA": KT + 4, "PB": KT + 8}
DU = {"OA": 2, "OB": 1, "F": 1, "PA": 1, "PB": 1}
LINKS = {"OA": 4, "OB": 5, "F": 5, "PA": 5, "PB": 5}
TICKS = 2 * UNITS
PLACES = [("S", 0, 0)] + [("O", n, 2 + 2 * n) for n in range(GROUPS + 1)] + [("LN", 0, 11), ("X", 0, 19)] + \
         [(k, f, 21 + 4 * f + d) for f in range(FT) for k, d in (("FG", 0), ("FU", 1), ("FH", 2), ("FD", 6))] + \
         [("LN", 1, 49), ("X", 1, 57)] + [(k, n, 59 + 4 * n + d) for n in range(4) for k, d in (("T", 0), ("W", 3))] + \
         [("V", 0, 74)]
PLACES.sort(key=lambda place: place[2])


class Count:

    def __init__(self, const, per=0):
        self.const, self.per = const, per

    def __add__(self, k):
        return Count(self.const + k.const, self.per + k.per) if isinstance(k, Count) else Count(self.const + k, self.per)

    def __mul__(self, k):
        return Count(self.const * k, self.per * k)

    def at(self, turn):
        return self.const + self.per * turn if isinstance(turn, int) or not self.per else turn * self.per + self.const


class Block:

    def __init__(self, name, seq, parity, before):
        self.name, self.seq, self.parity = name, seq, parity
        total = lambda w: sum((before[k] * w[k] for k in before), Count(0))
        self.gu, self.d, self.link = total(GU), total(DU), total(LINKS)
        self.ln = before["F"] + before["PA"] + before["PB"]
        self.o = before["OA"] + before["OB"]
        self.f = before["F"]
        self.p = before["PA"] + before["PB"]
        self.pb = before["PB"]


class Slot:
    def __init__(self, att, blocks, before):
        self.att, self.blocks = att, {}
        for name, seq, parity in blocks:
            self.blocks[name] = Block(name, seq, parity, dict(before))
            before[name] = before[name] + 1
        b = self.blocks
        self.out = b.get("OA") or b.get("OB")
        self.ffn = b.get("F")
        self.proj = b.get("PA") or b.get("PB")
        self.high_by_act = att is None or att[0] == "A"

    def steps(self, tick):
        for kind, n, at in PLACES:
            if kind in ("S", "O"):
                block = self.out
            elif kind[0] == "F" or kind in ("LN", "X") and n == 0:
                block = self.ffn
            else:
                block = self.proj
            if at == tick and block is not None and not (kind == "W" and block.name == "PA"):
                yield kind, n, block


def schedule():
    c = Count
    before = {k: c(0) for k in GU}
    first = [Slot(None, [("PA", c(0), 0)], before), Slot(("A", c(0), 0, None), [("PA", c(1), 1)], before)]
    ev, od, ev2, od2 = c(0, 2), c(1, 2), c(2, 2), c(3, 2)

    def turn(last):
        n = {"OA": c(0, 2), "OB": c(0, 2), "F": c(0, 4), "PB": c(0, 2), "PA": c(2, 2)}
        return [
            Slot(("A", od, 1, ("A", ev)), [("OA", ev, 0), ("F", ev, 0), ("PB", ev, 0)], n),
            Slot(("B", ev, 0, ("A", od)), [("OA", od, 1), ("F", od, 1), ("PB", od, 1)], n),
            Slot(("B", od, 1, ("B", ev)), [("OB", ev, 0), ("F", ev, 0)] + [("PA", ev2, 0)] * (not last), n),
            Slot(None if last else ("A", ev2, 0, ("B", od)),
                 [("OB", od, 1), ("F", od, 1)] + [("PA", od2, 1)] * (not last), n),
        ]

    return first, turn(False), turn(True)


def den_units(u):
    return range(u * DEN_UNITS // UNITS, (u + 1) * DEN_UNITS // UNITS)


def spread(ap, n):
    return bass.AP(tensor=ap.tensor, offset=ap.offset, ap=[list(x) for x in ap.ap] + [[0, n]])


def build(nc, x_in, Wq, bq, Wk, bk, Wv, bv, Wo, bo, Wqkv, Wout, bout, w_gate, w_up, w_down,
          cos_in, sin_in, masks_in, eye_in, sel_in, sums_in, swap_in, out):
    nc.disable_value_cache = True
    first, body, tail = schedule()
    ctx = ExitStack()
    with ctx:
        def sb(name, shape, dt):
            return ctx.enter_context(nc.sbuf_tensor(name, shape, dt))

        def sem(name):
            return ctx.enter_context(nc.semaphore(name))

        wa_qk = [sb(f"wa_qk{i}", [P, KT, 2 * D], F32R) for i in range(2)]
        wa_v = [sb(f"wa_v{i}", [P, KT, D], F32R) for i in range(2)]
        wa_o = [sb(f"wa_o{i}", [P, GROUPS, D], F32R) for i in range(2)]
        wb_qk = [sb(f"wb_qk{i}", [P, KT, 2 * D], F32R) for i in range(2)]
        wb_v = [sb(f"wb_v{i}", [P, KT, D], F32R) for i in range(2)]
        wb_o = [sb(f"wb_o{i}", [P, GROUPS, D], F32R) for i in range(2)]
        w_g = sb("w_g", [P, KT, HID], F32R)
        w_u = sb("w_u", [P, KT, HID], F32R)
        w_d = sb("w_d", [P, FT, D], F32R)
        cos = sb("cos", [P, S], F32)
        sin = sb("sin", [P, S], F32)
        mask0 = sb("mask0", [P, S], BF16)
        mask1 = sb("mask1", [P, 2 * WIDE[1]], BF16)
        mask3 = sb("mask3", [P, 2 * WIDE[3]], BF16)
        causal = sb("causal", [P, P], BF16)
        eye = sb("eye", [P, P], F32)
        eye_bf = sb("eye_bf", [P, P], BF16)
        swap = sb("swap", [P, P], F16)
        sel = sb("sel", [2 * HEADS, HEADS], BF16)
        sums_sel = sb("sums_sel", [P, GROUPS], F32)
        qk_bias = sb("qk_bias", [P, 4], F32)
        v_bias = sb("v_bias", [P, D], F32)
        o_bias = [sb(f"o_bias{i}", [P, D], F32) for i in range(2)]
        eps = sb("eps", [P, NT], F32)
        pause = sb("pause", [1, 1], F32)
        minus_half = sb("minus_half", [P, NT], F32)
        w_top = sb("w_top", [P, 1], F32)
        w_top1 = sb("w_top1", [1, 1], F32)
        general = sb("general", [1, 1], I32)
        x = [sb(f"x{i}", [P, NT, D], F32) for i in range(2)]
        xn = sb("xn", [P, NT, D], F32)
        xT = [sb(f"xT{i}", [P, KT, S], F32R) for i in range(2)]
        stats = sb("stats", [P, NT, 6], F32)
        mv = sb("mv", [P, NT, 2], F32)
        veps = sb("veps", [P, NT], F32)
        root = sb("root", [P, NT], F32)
        newton = sb("newton", [P, NT], F32)
        src = sb("src", [P, 2, 2, 2, 2, S], F16)
        pack = sb("pack", [P, 2, PACK], F16)
        v_aug = [sb(f"v_aug{i}", [P, NT, HEADS, DH + 1], F32) for i in range(2)]
        top = sb("top", [P, NT, HEADS], F32)
        ntop = sb("ntop", [P, NT, 2 * HEADS], BF16)
        ntopT = sb("ntopT", [2 * HEADS, S], BF16)
        probs = sb("probs", [P, RING, S], F32)
        den = [sb(f"den{i}", [P, GROUPS, NT, 4], F32) for i in range(2)]
        rden = sb("rden", [P, GROUPS, NT, 4], F32)
        o_sb = sb("o_sb", [P, GROUPS, S], F32)
        on = [sb(f"on{i}", [P, S], F32R) for i in range(2)]
        tmp = sb("tmp", [P, 4, S], F32)
        h = [sb(f"h{i}", [P, 2, S], F32R) for i in range(2)]
        s_bank = [ctx.enter_context(nc.psum_tensor(f"s_bank{i}", [P, S], F32)) for i in range(3)]
        o_bank = ctx.enter_context(nc.psum_tensor("o_bank", [P, S], F32))
        gu_bank = [ctx.enter_context(nc.psum_tensor(f"gu_bank{i}", [P, S], F32)) for i in range(2)]
        d_bank = ctx.enter_context(nc.psum_tensor("d_bank", [P, NT, D], F32))

        def q_pack(b):
            return pack[:, b, 0:PAIRS * S].rearrange("p (n s) -> p n s", s=S)

        def k_pack(b):
            return pack[:, b, PAIRS * S:PACK].rearrange("p (n s) -> p n s", s=S)

        BUFFER = {("A", 0): 1, ("A", 1): 0, ("U", 0): 1, ("U", 1): 1, ("R", 0): 0, ("R", 1): 0}

        w_in = sem("w_in")
        c_in = sem("c_in")
        zeroed = sem("zeroed")
        w_f32 = sem("w_f32")
        w_turned = sem("w_turned")
        w_taken = sem("w_taken")
        w_raw = sem("w_raw")
        w_flag = sem("w_flag")
        prep = sem("prep")
        packed = {(k, i, j): sem(f"packed_{k}{i}{j}") for k in "AUR" for i in range(2) for j in range(GROUPS)}
        a1_scores = sem("a1_scores")
        a1_taken = sem("a1_taken")
        ntop_ready = sem("ntop_ready")
        ntop_turned = sem("ntop_turned")
        ntopT_ready = sem("ntopT_ready")
        top_link = sem("top_link")
        a_scores = sem("a_scores")
        a_exp = sem("a_exp")
        a_used = sem("a_used")
        a_out_taken = sem("a_out_taken")
        den_scores = sem("den_scores")
        den_exp = sem("den_exp")
        b_scores = sem("b_scores")
        b_exp = sem("b_exp")
        b_used = sem("b_used")
        b_out_taken = sem("b_out_taken")
        x_in_sem = [sem(f"x_in{i}") for i in range(2)]
        x_stored = [sem(f"x_stored{i}") for i in range(2)]
        gu_ready = sem("gu_ready")
        gu_taken = sem("gu_taken")
        d_ready = sem("d_ready")
        d_taken = sem("d_taken")
        link = sem("link")
        mv_ready = sem("mv_ready")
        pool_link = sem("pool_link")
        root_ready = sem("root_ready")
        xn_ready = sem("xn_ready")
        xT_high = sem("xT_high")
        biased = sem("biased")
        spread_ready = sem("spread_ready")
        on_ready = sem("on_ready")
        on_used = sem("on_used")
        tanh_ready = sem("tanh_ready")
        h_high = sem("h_high")
        h_ready = sem("h_ready")
        h_used = sem("h_used")
        qk_high = sem("qk_high")
        rot_sum = sem("rot_sum")
        rot_high = sem("rot_high")
        rot_ready = sem("rot_ready")

        st = pack[:, :, :].rearrange("p b n -> p (b n)").bitcast(F32)
        at = [0]

        def stage(*shape):
            n = int(np.prod(shape))
            a = st[:, at[0]:at[0] + n]
            at[0] += n
            names = "abc"[:len(shape)]
            return a.rearrange(f"p ({' '.join(names)}) -> p {' '.join(names)}", **dict(zip(names, shape)))

        st_qkv = [stage(KT, D) for _ in range(3)]
        st_o = stage(KT, D)
        st_ocols = stage(KT, GROUPS * P)
        st_bqkv = stage(KT, 3 * D)
        st_brows = stage(GROUPS, D)
        st_int = st[:, at[0]:at[0] + 3 * FT * D].bitcast(I32)
        st_f32 = stage(3 * FT * D)
        st_dT = stage(FT, D)
        st2 = src[:, :, :, :, :, :].rearrange("p a b c d s -> p (a b c d s)").bitcast(F32)
        st_gT = st2[:, 0:KT * HID].rearrange("p (k n) -> p k n", k=KT)
        st_uT = st2[:, KT * HID:2 * KT * HID].rearrange("p (k n) -> p k n", k=KT)
        all_banks = [b[:, :] for b in s_bank] + [o_bank[:, :]] + [b[:, :] for b in gu_bank] + \
                    [d_bank[:, 0:2, :].rearrange("p a b -> p (a b)"), d_bank[:, 2:4, :].rearrange("p a b -> p (a b)")]
        NW, NC = 12, 16

        block = ctx.enter_context(nc.Block())

        @block.sync
        def _(sp):
            for st_w, w in zip(st_qkv + [st_o], (Wq, Wk, Wv, Wo)):
                sp.dma_start(st_w, w.rearrange("(t p) n -> p t n", p=P)).then_inc(w_in, 16)
            sp.dma_start(st_bqkv, Wqkv.rearrange("(t p) n -> p t n", p=P)).then_inc(w_in, 16)
            for n, w in enumerate((w_gate, w_up, w_down)):
                rows = w.shape[0] // P
                dst = st_int[:, n * FT * D:(n + 1) * FT * D].rearrange("p (t n) -> p t n", t=rows)
                sp.dma_start(dst, w.rearrange("(t p) n -> p t n", p=P)).then_inc(w_in, 16)
            sp.wait_ge(zeroed, 2)
            for c in range(4):
                rows = Wout.rearrange("(t j r d) n -> t r d j n", t=2, j=GROUPS, r=2)[c // 2, c % 2]
                sp.dma_start(st_brows[32 * c:32 * c + DH], rows).then_inc(w_in, 16)
            for dst, a in ((cos, cos_in), (sin, sin_in), (eye, eye_in), (sums_sel, sums_in), (swap, swap_in)):
                sp.dma_start(dst[:, :], a).then_inc(c_in, 16)
            col = 0
            for m in (mask0, mask1, mask3, causal, eye_bf):
                n = m.shape[1]
                sp.dma_start(m[:, :], masks_in[:, col:col + n].bitcast(BF16)).then_inc(c_in, 16)
                col += n
            sp.dma_start(sel[:, :], sel_in.bitcast(BF16)).then_inc(c_in, 16)
            for n, b in enumerate((bq, bk)):
                sp.dma_start(qk_bias[:, 2 * n:2 * n + 2], b.rearrange("(t p) -> p t", p=P),
                             allow_slow_non_contiguous=True).then_inc(c_in, 16)
            for dst, b in ((v_bias, bv), (o_bias[0], bo), (o_bias[1], bout)):
                sp.dma_start(dst[:, :], b.partition_broadcast(P)).then_inc(c_in, 16)
            for i in range(2):
                sp.dma_start(x[i][:, :, :], x_in[i].rearrange("(t p) n -> p t n", p=P)).then_inc(x_in_sem[i], 16)
            for n, (dst, a) in enumerate(((w_g, st_gT), (w_u, st_uT), (w_d, st_dT))):
                sp.wait_ge(w_taken, (9, 13, 16)[n])
                sp.dma_start(dst[:, :, :].bitcast(F32), a).then_inc(w_raw, 16)

            def load_pack(kind, parity):
                b, rotated = BUFFER[kind, parity], int(kind == "R")
                qp, kp = q_pack(b), k_pack(b)
                for j in range(GROUPS):
                    for n in range(4):
                        r = slice(32 * j, 32 * j + 32)
                        sp.dma_start(qp[32 * n:32 * n + 32, 2 * j:2 * j + 2, :], src[r, rotated, 0, n // 2, :, :])\
                            .then_inc(packed[kind, parity, j], 16)
                        for e in range(2):
                            r = slice(32 * j + DH * e, 32 * j + DH * e + DH)
                            sp.dma_start(kp[32 * n + DH * e:32 * n + DH * e + DH, 4 * j + e:4 * j + e + 3:2, :],
                                         src[r, rotated, 1, n % 2, :, :]).then_inc(packed[kind, parity, j], 16)

            def slot(s, turn):
                if s.att and s.att[0] == "B":
                    _, seq, parity, _ = s.att
                    sp.wait_ge(rot_ready, (seq * 4 + 4).at(turn))
                    if parity == 0:
                        sp.wait_ge(a_scores, ((seq + 2) * UNITS).at(turn))
                    else:
                        sp.wait_ge(b_scores, (seq * UNITS).at(turn))
                    load_pack("R", parity)
                if s.out and s.out.name == "OB":
                    seq, parity = s.ffn.seq, s.ffn.parity
                    sp.wait_ge(d_taken, (s.ffn.d + 1).at(turn))
                    sp.dma_start(out[bass.ds(seq.at(turn), 1)].rearrange("a (t p) n -> p (a t) n", p=P),
                                 x[parity][:, :, :]).then_inc(x_stored[parity], 16)
                    if s.proj:
                        sp.wait_ge(x_stored[parity], Count(16, 16).at(turn))
                        sp.dma_start(x[parity][:, :, :],
                                     x_in[bass.ds((seq + 2).at(turn), 1)].rearrange("a (t p) n -> p (a t) n", p=P))\
                            .then_inc(x_in_sem[parity], 16)
                if s.proj:
                    name, seq, parity = s.proj.name, s.proj.seq, s.proj.parity
                    sp.wait_ge(gu_taken, (s.proj.gu + (KT + (4 if name == "PA" else 7))).at(turn))
                    if name == "PB" and parity == 0:
                        sp.wait_ge(a_scores, ((seq + 1) * UNITS).at(turn))
                    elif name == "PB":
                        sp.wait_ge(den_scores, (seq * DEN_UNITS).at(turn))
                    elif parity == 0 and seq.per:
                        sp.wait_ge(den_scores, (seq * DEN_UNITS).at(turn))
                    elif seq.per:
                        sp.wait_ge(b_scores, ((seq + -1) * UNITS).at(turn))
                    else:
                        sp.wait_ge(zeroed, 3)
                    load_pack("U" if name == "PB" else "A", parity)

            for s in first:
                slot(s, 0)
            with sp.Fori(0, SEQS // 2 - 1) as turn:
                for s in body:
                    slot(s, turn)
            for s in tail:
                slot(s, SEQS // 2 - 1)
            for i in range(2):
                sp.wait_ge(x_stored[i], 16 * SEQS // 2)

        @block.tensor
        def _(pe):
            banks = []
            for n in range(3):
                banks.append([(k * D + t * P, st_qkv[n][:, t, k * P:(k + 1) * P]) for k in range(KT) for t in range(KT)])
            for half in range(2):
                banks.append([(j * D + t * P, st_ocols[:, t, (2 * half + j) * P:(2 * half + j + 1) * P])
                              for j in range(2) for t in range(KT)])
            for n in range(2):
                w = st_f32[:, n * FT * D:(n + 1) * FT * D].rearrange("p (t n) -> p t n", t=FT)
                for k in range(KT):
                    for half in range(2):
                        banks.append([(t * P, w[:, 3 * half + t, k * P:(k + 1) * P]) for t in range(3)])
            w = st_f32[:, 2 * FT * D:].rearrange("p (t n) -> p t n", t=KT)
            for pair in range(FT // 2):
                banks.append([(f * D + t * P, w[:, t, (2 * pair + f) * P:(2 * pair + f + 1) * P])
                              for f in range(2) for t in range(KT)])
            pe.wait_ge(c_in, 16 * NC)
            pe.wait_ge(w_in, 16 * NW)
            pe.wait_ge(w_f32, 2)
            for n, bank in enumerate(banks):
                if n >= len(all_banks):
                    pe.wait_ge(w_taken, n - len(all_banks) + 1)
                for c0, a in bank:
                    last = pe.transpose(all_banks[n % len(all_banks)][:, c0:c0 + P], a, eye[:, :])
                last.then_inc(w_turned, 1)
            pe.wait_ge(w_taken, len(banks))
            pe.wait_ge(w_flag, 1)
            pe.transpose(gu_bank[0][0:1, 0:P], w_top[:, :], eye[:, :]).then_inc(w_turned, 1)
            pe.wait_ge(w_flag, 3)
            pe.wait_ge(w_raw, 48)
            pe.wait_ge(zeroed, 3)
            is_general = pe.value_load(general[0:1, 0:1], min_val=0, max_val=1)

            def unit_bank(u):
                return s_bank[u % 3]

            def split_passes(lhs, rhs):
                return ((lhs[0], rhs[0]), (lhs[1], rhs[0]), (lhs[0], rhs[1]))

            def outputs_taken(s, turn, j):
                kind, seq, parity, prev = s.att
                if j:
                    pe.wait_ge(a_out_taken if kind == "A" else b_out_taken, (seq * GROUPS + j).at(turn))
                elif prev:
                    kind, pseq = prev
                    pe.wait_ge(a_out_taken if kind == "A" else b_out_taken, ((pseq + 1) * GROUPS).at(turn))

            def value(parity, j, c, t, n):
                return v_aug[parity][:, t, 8 * (c // 2) + 2 * j + c % 2, 0:n]

            def a_unit(s, turn, u, by_key):
                _, seq, parity, prev = s.att
                qp, kp = q_pack(BUFFER["A", parity]), k_pack(BUFFER["A", parity])
                j, n = divmod(u, NU)
                if not by_key and n == 0:
                    per_turn = seq.per // 2
                    pe.wait_ge(packed["A", parity, j],
                               Count(SETDMA * (seq.const // 2 + 1), SETDMA * per_turn).at(turn))
                if not by_key and u == 0 and prev:
                    kind, pseq = prev
                    pe.wait_ge(a_exp if kind == "A" else b_exp, ((pseq + 1) * UNITS).at(turn))
                if by_key and u == 0:
                    pe.wait_ge(ntopT_ready, (seq + 1).at(turn))
                if u >= 3:
                    pe.wait_ge(a_exp if by_key else a1_taken, (seq * UNITS + (u - 2)).at(turn))
                bank = unit_bank(u)
                mask = (mask0, mask1, mask3)[BATCH_OF[n]]
                pe.matmul(bank[:, 0:mask.shape[1]], eye_bf[:, :], mask[:, :], start=True, stop=False, skip_group_check=True)
                for c, t, c0 in UNITS_A[n]:
                    hh, pair = 4 * j + c, 2 * j + c // 2
                    stat = (kp[:, hh, :] if by_key else qp[:, pair, :])[:, t * P:(t + 1) * P]
                    moving = qp[:, pair, :] if by_key else kp[:, hh, :]
                    a, b = WINDOW[t]
                    pieces = [(c0, a, b)] + ([(c0 + b - a, 0, GLOBALS)] if t else [])
                    for col, a, b in pieces:
                        last = pe.matmul(bank[:, col:col + b - a], stat, moving[:, a:b], start=False, stop=not by_key,
                                         skip_group_check=True)
                    if by_key:
                        for col, a, b in pieces:
                            last = pe.matmul(bank[:, col:col + b - a], spread(sel[:, hh], P), ntopT[:, a:b],
                                             start=False, stop=True, skip_group_check=True)
                last.then_inc(a_scores if by_key else a1_scores, 1)

            def a_values(s, turn, j, batch):
                _, seq, parity, _ = s.att
                if batch == 0:
                    outputs_taken(s, turn, j)
                pe.wait_ge(a_exp, (seq * UNITS + (j * NU + BATCHES[batch][-1] + 1)).at(turn))
                pieces = []
                for n in BATCHES[batch]:
                    for c, t, c0 in UNITS_A[n]:
                        a, b = WINDOW[t]
                        pieces.append((t, 0, c, n, c0, a, b))
                        if t:
                            pieces.append((t, 1, c, n, c0 + b - a, 0, GLOBALS))
                for t, _, c, n, col, a, b in sorted(pieces):
                    last = pe.matmul(o_bank[32 * c:32 * c + DH + 1, a:b], value(parity, j, c, t, DH + 1),
                                     probs[:, (j * NU + n) % RING, col:col + b - a], start=t == 0, stop=t == NT - 1,
                                     tile_position=(0, 32 * c), skip_group_check=True)
                last.then_inc(a_used, 1)

            def turn_maxima(s, turn):
                _, seq, parity, _ = s.att
                pe.wait_ge(ntop_ready, (seq + 1).at(turn))
                for t in range(NT):
                    last = pe.matmul(unit_bank(0)[0:2 * HEADS, t * P:(t + 1) * P], ntop[:, t, :], eye_bf[:, :],
                                     start=True, stop=True)
                last.then_inc(ntop_turned, 1)

            def den_unit(s, turn, u):
                _, seq, parity, prev = s.att
                qp, kp = q_pack(BUFFER["U", parity]), k_pack(BUFFER["U", parity])
                hh, t = divmod(u, NT)
                if u % (4 * NT) == 0:
                    pe.wait_ge(packed["U", parity, hh // 4], Count(SETDMA, SETDMA).at(turn))
                if u == 0:
                    kind, pseq = prev
                    pe.wait_ge(a_exp if kind == "A" else b_exp, ((pseq + 1) * UNITS).at(turn))
                if u >= 3:
                    pe.wait_ge(den_exp, (seq * DEN_UNITS + (u - 2)).at(turn))
                pe.matmul(unit_bank(u)[:, :], qp[:, hh // 2, t * P:(t + 1) * P], kp[:, hh, :],
                          start=True, stop=True).then_inc(den_scores, 1)

            def b_unit(s, turn, u):
                _, seq, parity, _ = s.att
                qp, kp = q_pack(BUFFER["R", parity]), k_pack(BUFFER["R", parity])
                j, n = divmod(u, NU)
                if n == 0:
                    pe.wait_ge(packed["R", parity, j], Count(SETDMA, SETDMA).at(turn))
                if u == 0:
                    pe.wait_ge(den_exp, ((seq + 1) * DEN_UNITS).at(turn))
                if u >= 3:
                    pe.wait_ge(b_exp, (seq * UNITS + (u - 2)).at(turn))
                bank = unit_bank(u)
                for i, (c, t, c0) in enumerate(UNITS_B[n]):
                    pe.matmul(bank[:, c0:c0 + P], eye_bf[:, :], causal[:, :], start=i == 0, stop=False,
                              skip_group_check=True)
                for c, t, c0 in UNITS_B[n]:
                    last = pe.matmul(bank[:, c0:c0 + S - t * P], kp[:, 4 * j + c, t * P:(t + 1) * P],
                                     qp[:, 2 * j + c // 2, t * P:S], start=False, stop=True, skip_group_check=True)
                last.then_inc(b_scores, 1)

            def b_values(s, turn, j, batch):
                _, seq, parity, _ = s.att
                if batch == 0:
                    outputs_taken(s, turn, j)
                pe.wait_ge(b_exp, (seq * UNITS + (j * NU + BATCHES[batch][-1] + 1)).at(turn))
                pieces = [(t, c, n, c0) for n in BATCHES[batch] for c, t, c0 in UNITS_B[n]]
                for t, c, n, c0 in sorted(pieces):
                    last = pe.matmul(o_bank[32 * c:32 * c + DH, t * P:S], value(parity, j, c, t, DH),
                                     probs[:, (j * NU + n) % RING, c0:c0 + S - t * P], start=t == 0, stop=t == 2,
                                     tile_position=(0, 32 * c), skip_group_check=True)
                last.then_inc(b_used, 1)

            def gu(block, k, turn):
                if (block.gu + (k - 1)).const > 0:
                    pe.wait_ge(gu_taken, (block.gu + (k - 1)).at(turn))
                return gu_bank[k % 2]

            def sums(block, turn):
                pe.wait_ge(d_taken, block.d.at(turn))
                if block.name == "OA":
                    pe.wait_ge(a_out_taken, ((block.seq + 1) * GROUPS).at(turn))
                    for j in range(GROUPS):
                        for t in range(NT):
                            k = (j * NT + t) * 4
                            last = pe.matmul(d_bank[:, 0, k:k + 4], o_sb[:, j, t * P:(t + 1) * P], sums_sel[:, :],
                                             start=True, stop=True)
                    last.then_inc(d_ready, 1)

            def out_step(block, n, turn):
                w = wa_o if block.name == "OA" else wb_o
                if n < GROUPS:
                    bank = gu(block, n, turn)
                    pe.wait_ge(spread_ready, (block.o * GROUPS + (n + 1)).at(turn))
                    for t in range(NT):
                        last = pe.transpose(bank[:, t * P:(t + 1) * P], tmp[:, n % 2, t * P:(t + 1) * P], eye[:, :])
                    last.then_inc(gu_ready, 1)
                if n >= 1:
                    j = n - 1
                    if n == 1 and block.name == "OA":
                        pe.wait_ge(d_taken, (block.d + 1).at(turn))
                    pe.wait_ge(on_ready, (block.o * GROUPS + n).at(turn))
                    for t in range(NT):
                        for i, (a, b) in enumerate(split_passes(on, w)):
                            last = pe.matmul(d_bank[:, t, :], a[:, t * P:(t + 1) * P], b[:, j, :],
                                             start=j == 0 and i == 0 and t % 2 == 0, stop=j == GROUPS - 1 and i == 2,
                                             skip_group_check=True)
                    last.then_inc(d_ready if n == GROUPS else on_used, 1)

            def turn_x(block, turn):
                pe.wait_ge(xn_ready, (block.ln + 1).at(turn))
                for k in range(KT):
                    bank = gu(block, k, turn)
                    for t in range(NT):
                        last = pe.transpose(bank[:, t * P:(t + 1) * P], xn[:, t, k * P:(k + 1) * P], eye[:, :])
                    last.then_inc(gu_ready, 1)

            def plain(a, exact):
                return a if exact else a.bitcast(F32)

            def ffn_up(block, f, up, turn, exact):
                done = 2 * f + up - 1 if f or up else 0
                pe.wait_ge(gu_taken, (block.gu + (KT + done)).at(turn))
                w = w_u if up else w_g
                for k in range(KT):
                    for i in range(2):
                        last = pe.matmul(gu_bank[up][:, :], plain(w[:, k, f * P:(f + 1) * P], exact), plain(xT[i][:, k, :], exact),
                                         start=k == 0 and i == 0, stop=k == KT - 1 and i == 1)
                last.then_inc(gu_ready, 1)

            def ffn_down(block, f, turn, exact):
                if f == 0:
                    pe.wait_ge(d_taken, block.d.at(turn))
                pe.wait_ge(h_ready, (block.f * FT + (f + 1)).at(turn))
                for t in range(NT):
                    for i in range(2):
                        last = pe.matmul(d_bank[:, t, :], plain(h[i][:, f % 2, t * P:(t + 1) * P], exact),
                                         plain(w_d[:, f, :], exact), start=f == 0 and i == 0 and t % 2 == 0,
                                         stop=f == FT - 1 and i == 1, skip_group_check=True)
                last.then_inc(d_ready if f == FT - 1 else h_used, 1)

            def qk_step(block, n, turn):
                pa = block.name == "PA"
                if n == 0:
                    pe.wait_ge(gu_taken, (block.gu + KT).at(turn))
                bank = gu(block, KT + (n if pa else 2 * n), turn)
                for k in range(KT):
                    for i, (a, b) in enumerate(split_passes(wa_qk if pa else wb_qk, xT)):
                        last = pe.matmul(bank[:, :], a[:, k, n * P:(n + 1) * P], b[:, k, :],
                                         start=k == 0 and i == 0, stop=k == KT - 1 and i == 2)
                last.then_inc(gu_ready, 1)

            def swap_step(block, n, turn):
                pe.wait_ge(gu_taken, (block.gu + (KT + 2 * n + 1)).at(turn))
                for i in range(2):
                    last = pe.matmul(gu_bank[1][:, :], swap[:, :], src[:, 0, n // 2, i, n % 2, :], start=i == 0, stop=i == 1)
                last.then_inc(gu_ready, 1)

            def v_step(block, turn):
                w = wa_v if block.name == "PA" else wb_v
                if block.d.const:
                    pe.wait_ge(d_taken, block.d.at(turn))
                for t in range(NT):
                    for k in range(KT):
                        for i, (a, b) in enumerate(split_passes(xT, w)):
                            last = pe.matmul(d_bank[:, t, :], a[:, k, t * P:(t + 1) * P], b[:, k, :],
                                             start=k == 0 and i == 0 and t % 2 == 0, stop=k == KT - 1 and i == 2,
                                             skip_group_check=True)
                last.then_inc(d_ready, 1)

            def slot(s, turn, exact):
                values = {"A": a_values, "B": b_values}
                for tick in range(TICKS):
                    second, u = divmod(tick, UNITS)
                    if s.att:
                        kind = s.att[0]
                        if kind == "A":
                            if second and u == 0:
                                turn_maxima(s, turn)
                            a_unit(s, turn, u, second)
                        elif second:
                            b_unit(s, turn, u)
                        else:
                            for d in den_units(u):
                                den_unit(s, turn, d)
                        if second and u >= LAG and (u - LAG) % NU in [b[-1] for b in BATCHES]:
                            values[kind](s, turn, (u - LAG) // NU, BATCH_OF[(u - LAG) % NU])
                    for kind, n, block in s.steps(tick):
                        if kind == "S":
                            sums(block, turn)
                        elif kind == "O":
                            out_step(block, n, turn)
                        elif kind == "X":
                            turn_x(block, turn)
                        elif kind in ("FG", "FU"):
                            ffn_up(block, n, int(kind == "FU"), turn, exact)
                        elif kind == "FD":
                            ffn_down(block, n, turn, exact)
                        elif kind == "T":
                            qk_step(block, n, turn)
                        elif kind == "W":
                            swap_step(block, n, turn)
                        elif kind == "V":
                            v_step(block, turn)
                if s.att:
                    values[s.att[0]](s, turn, GROUPS - 1, len(BATCHES) - 1)

            def slots(exact):
                for s in first:
                    slot(s, 0, exact)
                with pe.Fori(0, SEQS // 2 - 1) as turn:
                    for s in body:
                        slot(s, turn, exact)
                for s in tail:
                    slot(s, SEQS // 2 - 1, exact)

            with pe.If(is_general > 0):
                slots(False)
            with pe.Else():
                slots(True)

        @block.scalar
        def _(act):
            def exp(s, turn, u):
                kind, seq, parity, prev = s.att
                scores, done, used = (a_scores, a_exp, a_used) if kind == "A" else (b_scores, b_exp, b_used)
                j, n = divmod(u, NU)
                width = (S, 2 * WIDE[1], 2 * WIDE[3])[BATCH_OF[n]] if kind == "A" else S
                if u == 0 and prev:
                    pkind, pseq = prev
                    act.wait_ge(a_used if pkind == "A" else b_used, ((pseq + 1) * USES).at(turn))
                act.wait_ge(scores, (seq * UNITS + (u + 1)).at(turn))
                if u >= RING:
                    pj, pn = divmod(u - RING, NU)
                    act.wait_ge(used, (seq * USES + (pj * len(BATCHES) + BATCH_OF[pn] + 1)).at(turn))
                act.activation(probs[:, u % RING, 0:width], s_bank[u % 3][:, 0:width], ACT.Exp, scale=SM_SCALE)\
                    .then_inc(done, 1)

            def den_exponential(s, turn, u):
                _, seq, parity, _ = s.att
                hh, t = divmod(u, NT)
                act.wait_ge(den_scores, (seq * DEN_UNITS + (u + 1)).at(turn))
                act.activation(probs[:, u % 3, 0:S // 2].bitcast(BF16), s_bank[u % 3][:, :], ACT.Exp, scale=SM_SCALE,
                               accum_out=den[parity][:, hh // 4, t, hh % 4:hh % 4 + 1]).then_inc(den_exp, 1)

            def x_high(block, turn):
                for k in range(KT):
                    act.wait_ge(gu_ready, (block.gu + (k + 1)).at(turn))
                    act.activation(xT[0][:, k, :], gu_bank[k % 2][:, :], ACT.Copy).then_inc(xT_high, 1)

            def half_tanh(block, f, turn):
                if f >= 2:
                    act.wait_ge(h_ready, (block.f * FT + (f - 1)).at(turn))
                act.wait_ge(gu_ready, (block.gu + (KT + 2 * f + 1)).at(turn))
                act.activation(tmp[:, f % 2, :], gu_bank[0][:, :], ACT.Tanh, scale=0.5 * DEQUANT).then_inc(tanh_ready, 1)

            def high(block, f, turn):
                act.wait_ge(gu_taken, (block.gu + (KT + 2 * f + 2)).at(turn))
                if f >= 2:
                    act.wait_ge(h_used, (block.f * (FT - 1) + (f - 1)).at(turn))
                act.activation(h[0][:, f % 2, :], tmp[:, f % 2, :], ACT.Copy).then_inc(h_high, 1)

            def qk_step(block, n, att, turn):
                pa = block.name == "PA"
                k = KT + (n if pa else 2 * n)
                act.wait_ge(gu_ready, (block.gu + (k + 1)).at(turn))
                dst = src[:, 0, n // 2, 0, n % 2, :]
                if pa:
                    act.activation(dst, gu_bank[k % 2][:, :], ACT.Identity, bias=qk_bias[:, n:n + 1]).then_inc(qk_high, 1)
                else:
                    act.activation(dst, gu_bank[k % 2][:, :], ACT.Copy).then_inc(qk_high, 1)

            def rot_high_step(block, n, att, turn):
                if n == 0 and att[0] == "B":
                    for j in range(GROUPS):
                        act.wait_ge(packed["R", att[2], j], Count(SETDMA, SETDMA).at(turn))
                act.wait_ge(rot_sum, (block.seq * 4 + (n + 1)).at(turn))
                act.activation(src[:, 1, n // 2, 0, n % 2, :], tmp[:, 2 * (n % 2), :], ACT.Copy).then_inc(rot_high, 1)

            def slot(s, turn):
                for tick in range(TICKS):
                    second, u = divmod(tick, UNITS)
                    if s.att and second:
                        if s.att[0] == "A" and u == 0:
                            act.wait_ge(ntop_turned, (s.att[1] + 1).at(turn))
                            act.activation(ntopT[:, :], s_bank[0][0:2 * HEADS, :], ACT.Copy).then_inc(ntopT_ready, 1)
                        exp(s, turn, u)
                    elif s.att and s.att[0] == "B":
                        for d in den_units(u):
                            den_exponential(s, turn, d)
                    for kind, n, block in s.steps(tick):
                        if kind == "X":
                            x_high(block, turn)
                        elif kind == "FG":
                            half_tanh(block, n, turn)
                        elif kind == "FH" and s.high_by_act:
                            high(block, n, turn)
                        elif kind == "T":
                            qk_step(block, n, s.att, turn)
                        elif kind == "W":
                            rot_high_step(block, n, s.att, turn)

            act.wait_ge(c_in, 16 * NC)
            act.wait_ge(w_raw, 48)
            for s in first:
                slot(s, 0)
            with act.Fori(0, SEQS // 2 - 1) as turn:
                for s in body:
                    slot(s, turn)
            for s in tail:
                slot(s, SEQS // 2 - 1)

        @block.vector
        def _(dve):
            done = [0]

            def then(ins):
                done[0] += 1
                ins.then_inc(prep, 1)
                dve.wait_ge(prep, done[0])

            def split(parts, a):
                then(dve.tensor_copy(parts[0], a))
                return dve.tensor_tensor(parts[1], a, parts[0].bitcast(F32), ALU.subtract)

            dve.memset(st_ocols, 0.0).then_inc(zeroed, 1)
            dve.memset(st_brows, 0.0).then_inc(zeroed, 1)
            dve.wait_ge(zeroed, 2)
            dve.wait_ge(w_in, 16 * NW)
            for t in range(KT):
                for c in range(2):
                    dst = st_ocols[:, t, :].rearrange("p (j a r d) -> p j a r d", j=GROUPS, a=2, r=2)[:, :, c, :, 0:DH]
                    a = st_o[:, t, :].rearrange("p (a j r d) -> p a j r d", a=2, j=GROUPS, r=2)[:, c, :, :, :]
                    last = dve.tensor_copy(dst, a)
            last.then_inc(w_f32, 1)
            dve.tensor_copy(st_f32, st_int).then_inc(w_f32, 1)
            dve.wait_ge(w_f32, 2)
            dve.tensor_reduce(w_top[:, :], st_f32, axis=AX.X, op=ALU.max, apply_absolute_value=True).then_inc(w_flag, 1)
            split([w[:, :, :] for w in wb_qk], st_bqkv[:, :, 0:2 * D])
            split([w[:, :, :] for w in wb_v], st_bqkv[:, :, 2 * D:3 * D])
            split([w[:, :, :] for w in wb_o], st_brows)
            for n in range(16):
                dve.wait_ge(w_turned, n + 1)
                bank = all_banks[n % len(all_banks)]
                if n < 3:
                    w, c = ((wa_qk, 0), (wa_qk, D), (wa_v, 0))[n]
                    split([a[:, :, c:c + D] for a in w], bank.rearrange("p (k n) -> p k n", k=KT)).then_inc(w_taken, 1)
                elif n < 5:
                    j = 2 * (n - 3)
                    split([a[:, j:j + 2, :] for a in wa_o], bank.rearrange("p (k n) -> p k n", k=2)).then_inc(w_taken, 1)
                elif n < 13:
                    dst, k, half = (st_gT, st_uT)[(n - 5) // 4], (n - 5) // 2 % 2, (n - 5) % 2
                    dve.tensor_copy(dst[:, k, half * 3 * P:(half + 1) * 3 * P], bank[:, 0:3 * P]).then_inc(w_taken, 1)
                else:
                    f = 2 * (n - 13)
                    dve.tensor_copy(st_dT[:, f:f + 2, :], bank.rearrange("p (k n) -> p k n", k=2)).then_inc(w_taken, 1)
            dve.wait_ge(w_turned, 17)
            dve.tensor_reduce(w_top1[:, :], gu_bank[0][0:1, 0:P], axis=AX.X, op=ALU.max).then_inc(w_flag, 1)
            dve.wait_ge(w_flag, 2)
            dve.tensor_single_scalar(general[:, :], w_top1[:, :], EXACT, ALU.is_gt).then_inc(w_flag, 1)
            dve.memset(o_bank[:, :], 0.0)
            for i in range(2):
                dve.memset(v_aug[i][:, :, :, :], 1.0)
            dve.wait_ge(w_raw, 48)
            dve.memset(pack[:, :, :].rearrange("p b n -> p (b n)").bitcast(F32), 0.0).then_inc(zeroed, 1)
            dve.wait_ge(zeroed, 3)

            def a_maxima(s, turn, u):
                _, seq, parity, _ = s.att
                j, n = divmod(u, NU)
                batch, hh = BATCH_OF[n], 4 * j + UNITS_A[n][0][0]
                bank = s_bank[u % 3]
                if batch == 0:
                    dst, a = top[:, 0, hh:hh + 1], bank[:, :]
                elif batch == 1:
                    dst, a = top[:, 1:3, hh], bank[:, 0:2 * WIDE[1]].rearrange("p (a b) -> p a b", a=2)
                else:
                    dst, a = top[:, 3, hh:hh + 2], bank[:, 0:2 * WIDE[3]].rearrange("p (a b) -> p a b", a=2)
                dve.wait_ge(a1_scores, (seq * UNITS + (u + 1)).at(turn))
                dve.reduce_max(dst, a, AX.X).then_inc(a1_taken, 1)

            def minus_maxima(s, turn):
                _, seq, parity, _ = s.att
                dve.wait_ge(a1_taken, ((seq + 1) * UNITS).at(turn))
                dve.tensor_scalar(ntop[:, :, 0:HEADS], top[:, :, :], -1.0, None, ALU.mult).then_inc(top_link, 1)
                dve.wait_ge(top_link, (seq + 1).at(turn))
                dve.scalar_tensor_tensor(ntop[:, :, HEADS:2 * HEADS], top[:, :, :], -1.0, ntop[:, :, 0:HEADS],
                                         ALU.mult, ALU.subtract).then_inc(ntop_ready, 1)

            def take_out(s, turn, j):
                kind, seq, parity, _ = s.att
                used, taken = (a_used, a_out_taken) if kind == "A" else (b_used, b_out_taken)
                dve.wait_ge(used, (seq * USES + (j + 1) * len(BATCHES)).at(turn))
                dve.tensor_copy(o_sb[:, j, :], o_bank[:, :]).then_inc(taken, 1)

            def linked(block, n, ins, turn):
                ins.then_inc(link, 1)
                dve.wait_ge(link, (block.link + n).at(turn))

            def spread_group(block, j, turn):
                dst = tmp[:, j % 2, :].rearrange("p (a b) -> p a b", b=32)
                dve.tensor_copy(dst, spread(rden[:, j, :, :].rearrange("p t c -> p (t c)"), 32)).then_inc(spread_ready, 1)

            def reciprocals(block, turn):
                if block.pb.const:
                    dve.wait_ge(rot_ready, (block.pb * 4).at(turn))
                flat = rden[:, :, :, :].rearrange("p j t c -> p (j t c)")
                if block.name == "OA":
                    dve.wait_ge(d_ready, (block.d + 1).at(turn))
                    dve.reciprocal(flat, d_bank[:, 0, 0:4 * GROUPS * NT]).then_inc(d_taken, 1)
                    dve.wait_ge(d_taken, (block.d + 1).at(turn))
                else:
                    dve.wait_ge(den_exp, ((block.seq + 1) * DEN_UNITS).at(turn))
                    linked(block, 1, dve.reciprocal(flat, den[block.parity][:, :, :, :].rearrange("p j t c -> p (j t c)")), turn)
                spread_group(block, 0, turn)

            def out_step(block, n, turn):
                if n < GROUPS:
                    if n + 1 < GROUPS:
                        spread_group(block, n + 1, turn)
                    dve.wait_ge(gu_ready, (block.gu + (n + 1)).at(turn))
                    dve.tensor_tensor(o_sb[:, n, :], o_sb[:, n, :], gu_bank[n % 2][:, :], ALU.mult).then_inc(gu_taken, 1)
                    dve.wait_ge(gu_taken, (block.gu + (n + 1)).at(turn))
                    if n:
                        dve.wait_ge(on_used, (block.o * (GROUPS - 1) + n).at(turn))
                    linked(block, n + LINKS[block.name] - GROUPS + 1, dve.tensor_copy(on[0][:, :], o_sb[:, n, :]), turn)
                    dve.tensor_tensor(on[1][:, :], o_sb[:, n, :], on[0][:, :].bitcast(F32), ALU.subtract)\
                        .then_inc(on_ready, 1)
                else:
                    xs = x[block.parity][:, :, :]
                    dve.wait_ge(biased, block.p.at(turn))
                    dve.wait_ge(d_ready, (block.d + DU[block.name]).at(turn))
                    dve.tensor_tensor(xs, xs, d_bank[:, :, :], ALU.add).then_inc(d_taken, 1)
                    dve.wait_ge(d_taken, (block.d + DU[block.name]).at(turn))

            def normalise(block, turn):
                xs = x[block.parity]
                if block.name == "PA":
                    dve.wait_ge(x_in_sem[block.parity], (Count(16 * (block.seq.const // 2 + 1), 16 * (block.seq.per // 2))).at(turn))
                for t in range(NT):
                    ins = dve.bn_stats(stats[:, t, :], xs[:, t, :])
                linked(block, 1, ins, turn)
                dve.memset(pause[:, :], 0.0)
                for t in range(NT):
                    ins = dve.bn_aggr(mv[:, t, :], stats[:, t, :])
                ins.then_inc(mv_ready, 1)
                dve.wait_ge(root_ready, (block.ln + 1).at(turn))
                linked(block, 2, dve.tensor_tensor(newton[:, :], root[:, :], root[:, :], ALU.mult), turn)
                linked(block, 3, dve.tensor_tensor(newton[:, :], newton[:, :], veps[:, :], ALU.mult), turn)
                linked(block, 4, dve.tensor_scalar(newton[:, :], newton[:, :], -0.5, 1.5, ALU.mult, ALU.add), turn)
                linked(block, 5, dve.tensor_tensor(root[:, :], root[:, :], newton[:, :], ALU.mult), turn)
                for t in range(NT):
                    ins = dve.tensor_scalar(xn[:, t, :], xs[:, t, :], mv[:, t, 0:1], root[:, t:t + 1], ALU.subtract, ALU.mult)
                ins.then_inc(xn_ready, 1)

            def x_low(block, turn):
                for k in range(KT):
                    dve.wait_ge(xT_high, (block.ln * KT + (k + 1)).at(turn))
                    dve.tensor_tensor(xT[1][:, k, :], gu_bank[k % 2][:, :], xT[0][:, k, :].bitcast(F32), ALU.subtract)\
                        .then_inc(gu_taken, 1)
                    dve.wait_ge(gu_taken, (block.gu + (k + 1)).at(turn))

            def hidden(block, f, turn):
                t = tmp[:, f % 2, :]
                dve.wait_ge(tanh_ready, (block.f * FT + (f + 1)).at(turn))
                k = block.gu + (KT + 2 * f + 1)
                dve.scalar_tensor_tensor(t, t, 1.0, gu_bank[0][:, :], ALU.add, ALU.mult).then_inc(gu_taken, 1)
                dve.wait_ge(gu_taken, k.at(turn))
                dve.wait_ge(gu_ready, (k + 1).at(turn))
                dve.tensor_tensor(t, t, gu_bank[1][:, :], ALU.mult).then_inc(gu_taken, 1)

            def high(block, f, turn):
                dve.wait_ge(gu_taken, (block.gu + (KT + 2 * f + 2)).at(turn))
                if f >= 2:
                    dve.wait_ge(h_used, (block.f * (FT - 1) + (f - 1)).at(turn))
                dve.tensor_copy(h[0][:, f % 2, :], tmp[:, f % 2, :]).then_inc(h_high, 1)

            def add_ffn(block, turn):
                xs = x[block.parity][:, :, :]
                dve.wait_ge(d_ready, (block.d + 1).at(turn))
                dve.scalar_tensor_tensor(xs, d_bank[:, :, :], 0.5 * DEQUANT ** 3, xs, ALU.mult, ALU.add)\
                    .then_inc(d_taken, 1)
                dve.wait_ge(d_taken, (block.d + 1).at(turn))

            def qk_step(block, n, turn):
                pa = block.name == "PA"
                k = KT + (n if pa else 2 * n)
                dve.wait_ge(qk_high, (block.p * 4 + (n + 1)).at(turn))
                hi, lo = src[:, 0, n // 2, 0, n % 2, :], src[:, 0, n // 2, 1, n % 2, :]
                if pa:
                    dve.scalar_tensor_tensor(lo, gu_bank[k % 2][:, :], qk_bias[:, n:n + 1], hi, ALU.add, ALU.subtract)\
                        .then_inc(gu_taken, 1)
                else:
                    dve.tensor_tensor(lo, gu_bank[0][:, :], hi, ALU.subtract)
                    if n >= 2:
                        dve.wait_ge(rot_ready, (block.seq * 4 + (n - 1)).at(turn))
                    dve.tensor_tensor(tmp[:, 2 * (n % 2), :], gu_bank[0][:, :], cos[:, :], ALU.mult).then_inc(gu_taken, 1)

            def swap_step(block, n, turn):
                dve.wait_ge(gu_ready, (block.gu + (KT + 2 * n + 2)).at(turn))
                dve.tensor_tensor(tmp[:, 2 * (n % 2) + 1, :], gu_bank[1][:, :], sin[:, :], ALU.mult).then_inc(gu_taken, 1)

            def v_step(block, turn):
                dve.wait_ge(d_ready, (block.d + 1).at(turn))
                for t in range(NT):
                    dst = v_aug[block.parity][:, t, :, 0:DH]
                    a = d_bank[:, t, :].rearrange("p (h d) -> p h d", h=HEADS)
                    if block.name == "PA":
                        ins = dve.tensor_tensor(dst, a, v_bias[:, :].rearrange("p (h d) -> p h d", h=HEADS), ALU.add)
                    else:
                        ins = dve.tensor_copy(dst, a)
                ins.then_inc(d_taken, 1)

            def slot(s, turn):
                for tick in range(TICKS):
                    second, u = divmod(tick, UNITS)
                    if s.att and s.att[0] == "A" and not second:
                        a_maxima(s, turn, u)
                        if u == UNITS - 1:
                            minus_maxima(s, turn)
                    if s.att and second and u > NU and u % NU == LAG:
                        take_out(s, turn, u // NU - 1)
                    for kind, n, block in s.steps(tick):
                        if kind == "S":
                            reciprocals(block, turn)
                        elif kind == "O":
                            out_step(block, n, turn)
                        elif kind == "LN":
                            normalise(block, turn)
                        elif kind == "X":
                            x_low(block, turn)
                        elif kind == "FU":
                            hidden(block, n, turn)
                        elif kind == "FH" and not s.high_by_act:
                            high(block, n, turn)
                        elif kind == "FD" and n == FT - 1:
                            add_ffn(block, turn)
                        elif kind == "T":
                            qk_step(block, n, turn)
                        elif kind == "W":
                            swap_step(block, n, turn)
                        elif kind == "V":
                            v_step(block, turn)
                if s.att:
                    take_out(s, turn, GROUPS - 1)

            for s in first:
                slot(s, 0)
            with dve.Fori(0, SEQS // 2 - 1) as turn:
                for s in body:
                    slot(s, turn)
            for s in tail:
                slot(s, SEQS // 2 - 1)

        @block.gpsimd
        def _(pool):
            pool.memset(minus_half[:, :], -0.5).then_inc(pool_link, 1)
            pool.memset(eps[:, :], EPS).then_inc(pool_link, 1)
            pool.wait_ge(pool_link, 2)
            pool.wait_ge(c_in, 16 * NC)

            def rsqrt(block, turn):
                pool.wait_ge(mv_ready, (block.ln + 1).at(turn))
                pool.tensor_tensor(veps[:, :], mv[:, :, 1], eps[:, :], ALU.add).then_inc(pool_link, 1)
                pool.wait_ge(pool_link, (block.ln + 3).at(turn))
                pool.tensor_tensor(root[:, :], veps[:, :], minus_half[:, :], ALU.pow).then_inc(root_ready, 1)

            def add_bias(block, turn):
                pool.wait_ge(xn_ready, (block.ln + 1).at(turn))
                xs = x[block.parity]
                for t in range(NT):
                    ins = pool.tensor_tensor(xs[:, t, :], xs[:, t, :], o_bias[block.name == "PB"][:, :], ALU.add)
                ins.then_inc(biased, 1)

            def ffn_step(block, f, turn):
                pool.wait_ge(h_high, (block.f * FT + (f + 1)).at(turn))
                pool.tensor_tensor(h[1][:, f % 2, :], tmp[:, f % 2, :], h[0][:, f % 2, :].bitcast(F32), ALU.subtract)\
                    .then_inc(h_ready, 1)

            def rotate(block, n, turn):
                t = 2 * (n % 2)
                pool.wait_ge(gu_taken, (block.gu + (KT + 2 * n + 2)).at(turn))
                pool.tensor_tensor(tmp[:, t, :], tmp[:, t, :], tmp[:, t + 1, :], ALU.add).then_inc(rot_sum, 1)
                pool.wait_ge(rot_high, (block.seq * 4 + (n + 1)).at(turn))
                pool.tensor_tensor(src[:, 1, n // 2, 1, n % 2, :], tmp[:, t, :], src[:, 1, n // 2, 0, n % 2, :], ALU.subtract)\
                    .then_inc(rot_ready, 1)

            def slot(s, turn):
                for tick in range(TICKS):
                    for kind, n, block in s.steps(tick):
                        if kind == "LN":
                            rsqrt(block, turn)
                            if block.name != "F":
                                add_bias(block, turn)
                        elif kind == "FH":
                            ffn_step(block, n, turn)
                        elif kind == "W":
                            rotate(block, n, turn)

            for s in first:
                slot(s, 0)
            with pool.Fori(0, SEQS // 2 - 1) as turn:
                for s in body:
                    slot(s, turn)
            for s in tail:
                slot(s, SEQS // 2 - 1)


def shape_constants():
    i = np.arange(DH // 2, dtype=np.float32)
    theta = np.power(np.float32(10000.0), np.float32(-2.0) * (i - np.float32(1.0)) / np.float32(DH)).astype(np.float32)
    angle = (np.arange(S, dtype=np.float32)[:, None] * theta[None, :]).astype(np.float32)
    d = np.arange(P) % DH
    cos = np.cos(angle)[:, d // 2].T
    sin = np.sin(angle)[:, d // 2].T * np.where(d % 2, 1.0, -1.0)[:, None]
    r = np.arange(P)[:, None]
    c = np.arange(S)[None, :]
    seen = (np.abs(r - c) <= HALF) | (c < GLOBALS) | (r < GLOBALS)
    masks = [np.where(seen, 0.0, MASKED)]
    for t in (1, 3):
        a, b = WINDOW[t]
        near = np.abs(r + t * P - np.arange(a, b)[None, :]) <= HALF
        near = np.concatenate([near, np.ones((P, GLOBALS), bool)], 1)
        masks.append(np.tile(np.where(near, 0.0, MASKED), (1, 2)))
    masks.append(np.where(r <= np.arange(P)[None, :], 0.0, MASKED))
    masks.append(np.eye(P))
    sel = (np.arange(2 * HEADS)[:, None] % HEADS == np.arange(HEADS)[None, :])
    sums = (np.arange(P)[:, None] == 32 * np.arange(GROUPS)[None, :] + DH)
    f = lambda a, t: np.ascontiguousarray(a, dtype=t)
    bf16 = lambda a: np.ascontiguousarray(f(a, np.float32).view(np.uint32) >> 16, dtype=np.uint16)
    return {"cos": f(cos, np.float32), "sin": f(sin, np.float32),
            "masks": bf16(np.concatenate(masks, 1)), "eye": f(np.eye(P), np.float32),
            "sel": bf16(sel), "sums": f(sums, np.float32), "swap": f(np.eye(P)[np.arange(P) ^ 1], np.float16)}


_INS = ["L0_attn_a_x", "L0_attn_a_Wq", "L0_attn_a_bq", "L0_attn_a_Wk", "L0_attn_a_bk", "L0_attn_a_Wv", "L0_attn_a_bv",
        "L0_attn_a_Wo", "L0_attn_a_bo", "L0_attn_b_Wqkv", "L0_attn_b_Wout", "L0_attn_b_bout", "L0_ffn_w_gate",
        "L0_ffn_w_up", "L0_ffn_w_down"]


def kernel(**inputs):
    import numpy as _np
    import concourse.bacc as _bacc
    from concourse import mybir as _mybir
    from concourse.bass_utils import run_bass_kernel_spmd as _run

    nc = _bacc.Bacc("TRN2", target_bir_lowering=False, num_devices=1)
    arrays, args = {}, []
    given = {n: _np.ascontiguousarray(inputs[n]) for n in _INS}
    for name, a in {**given, **shape_constants()}.items():
        arrays[f"in_{name}_dram"] = a
        args.append(nc.dram_tensor(f"in_{name}_dram", a.shape, _mybir.dt.from_np(a.dtype), kind="ExternalInput").ap())
    args.append(nc.dram_tensor("out_dram", (SEQS, S, D), _mybir.dt.float32, kind="ExternalOutput").ap())
    build(nc, *args)
    r = _run(nc, [arrays], core_ids=[0])
    return r.results[0]["out_dram"]
```

```python
import numpy as np
import concourse.bass as bass
from concourse import mybir
from concourse.alu_op_type import AluOpType as ALU
from contextlib import ExitStack

F32, F32R = mybir.dt.float32, mybir.dt.float32r
F16, BF16, I32 = mybir.dt.float16, mybir.dt.bfloat16, mybir.dt.int32
ACT = mybir.ActivationFunctionType
AX = mybir.AxisListType

SEQS, S, D = 16, 512, 256
HEADS, DH = 16, 16
HID = 768
P = 128
NT, KT, FT = S // P, D // P, HID // P
GROUPS = 4
PAIRS = HEADS // 2
PACK = HEADS // 2 * S + HEADS * S
HALF, GLOBALS = 32, 4
MASKED = -1e30
EPS = 1e-5
SM_SCALE = float(DH) ** -0.5
DEQUANT = float(np.float32(1.0 / 127.0))
EXACT = 2048.0

WINDOW = [(max(t * P - HALF, 0), min((t + 1) * P + HALF, S)) for t in range(NT)]
WINDOW[0] = (0, P + HALF + GLOBALS)
WIDE = [b - a + (GLOBALS if t else 0) for t, (a, b) in enumerate(WINDOW)]
UNITS_A = [[]] + [[(c, 0, 0), (c, 3, WIDE[0])] for c in range(4)] + [[(c, 1, 0), (c, 2, WIDE[1])] for c in range(4)]
UNITS_B = [[(c, 0, 0)] for c in range(4)] + [[(c, 1, 0), (c, 3, 3 * P)] for c in range(4)] + \
          [[(c, 2, 0), (c + 1, 2, 2 * P)] for c in (0, 2)]
WIDTH_A = [S] + [WIDE[0] + WIDE[3]] * 4 + [WIDE[1] + WIDE[2]] * 4
NU = {"A": len(UNITS_A), "B": len(UNITS_B)}
BATCHES = {"A": [(0,), (1, 2, 3, 4), (5, 6, 7, 8)], "B": [(0, 1, 2, 3), (4, 5, 6, 7), (8, 9)]}
LAGS = {"A": (4, 3, 2), "B": (2, 3, 2)}
BATCH_OF = {k: [b for b, units in enumerate(BATCHES[k]) for _ in units] for k in NU}
RING = 6
UNITS = {k: GROUPS * NU[k] for k in NU}
USES = GROUPS * 3
DEN_UNITS = HEADS * NT
SETDMA = 12 * 16
GU = {"OA": 2 + GROUPS, "OB": GROUPS, "F": 2 * FT, "PA": 4, "PB": 8, "VA": 0, "VB": 0}
DU = {"OA": 3, "OB": 2, "F": KT + 2, "PA": KT, "PB": KT, "VA": 1, "VB": 1}
LINKS = {"OA": 0, "OB": 1, "F": 4, "PA": 4, "PB": 4, "VA": 0, "VB": 0}
TICKS = 80
FIRST = {"A": 40, "B": 40}


def places(sums, o, norm, ffn, norm2, proj, v):
    at = [(k, n, sums[n]) for n in range(2) for k in ("S", "S1", "S2")]
    for n in range(GROUPS + 2):
        at += [("O", n, o[0] + o[1] * n), ("O1", n, o[0] + o[1] * n + 1), ("O2", n, o[0] + o[1] * n + 2)]
    for n, (first, turned) in enumerate((norm, norm2)):
        at += [(f"N{i}", n, first + d) for i, d in enumerate((0, 1, 3, 4, 5, 6))] + [("X", n, turned), ("X1", n, turned + 1)]
    for f in range(FT):
        at += [(k, f, ffn[0] + ffn[1] * f + d) for k, d in (("G", 0), ("U", 1), ("H", 2), ("I", 3), ("J", 4), ("D", ffn[2]))]
    for n in range(4):
        at += [(k, n, proj[0] + proj[1] * n + d) for k, d in (("T", 0), ("T1", 1), ("T2", 2), ("W", proj[2]), ("W1", proj[2] + 1), ("W2", proj[2] + 3))]
    at += [("V", 0, v[0]), ("V1", 0, v[1])]
    return sorted(at, key=lambda place: place[2])


PLACES = {"A": places(sums=(78, -1), o=(-1, 2), norm=(11, 19), ffn=(23, 3, 6), norm2=(45, 53), proj=(57, 4, 4), v=(13, 14)),
          "B": places(sums=(78, -1), o=(-1, 2), norm=(11, 19), ffn=(21, 3, 6), norm2=(43, 51), proj=(53, 5, 4), v=(11, 14))}


class Count:

    def __init__(self, const, per=0):
        self.const, self.per = const, per

    def __add__(self, k):
        return Count(self.const + k.const, self.per + k.per) if isinstance(k, Count) else Count(self.const + k, self.per)

    def __mul__(self, k):
        return Count(self.const * k, self.per * k)

    def at(self, turn):
        return self.const + self.per * turn if isinstance(turn, int) or not self.per else turn * self.per + self.const


class Block:

    def __init__(self, name, seq, parity, before):
        self.name, self.seq, self.parity = name, seq, parity
        total = lambda w: sum((before[k] * w[k] for k in before), Count(0))
        self.gu, self.d, self.link = total(GU), total(DU), total(LINKS)
        self.ln = before["F"] + before["PA"] + before["PB"]
        self.o = before["OA"] + before["OB"]
        self.f = before["F"]
        self.p = before["PA"] + before["PB"]
        self.pb = before["PB"]


class Slot:
    def __init__(self, att, blocks, before):
        self.att, self.blocks, self.early = att, {}, None
        for name, seq, parity in blocks:
            self.blocks[name] = Block(name, seq, parity, dict(before))
            before[name] = before[name] + 1
        b = self.blocks
        self.out = b.get("OA") or b.get("OB")
        self.ffn = b.get("F")
        self.proj = b.get("PA") or b.get("PB")
        self.v = b.get("VA") or b.get("VB")

    def steps(self, tick):
        for kind, n, at in PLACES[self.att[0] if self.att else "A"]:
            if kind[0] in "SO":
                block = self.early if kind[0] == "S" and n == 0 else self.out
            elif kind[0] == "V":
                block = self.v
            elif kind in "GUHIJD" or kind[0] in "NX" and n == 0:
                block = self.ffn
            else:
                block = self.proj
            if at == tick and block is not None and not (kind[0] == "W" and block.name == "PA"):
                yield kind, n, block


def schedule():
    c = Count
    before = {k: c(0) for k in GU}
    first = [Slot(None, [("PA", c(0), 0)], before), Slot(("A", c(0), 0, None), [("VA", c(0), 0), ("PA", c(1), 1)], before)]
    ev, od, ev2, od2 = c(0, 2), c(1, 2), c(2, 2), c(3, 2)

    def counts():
        return {"OA": c(0, 2), "OB": c(0, 2), "F": c(0, 4), "PB": c(0, 2), "PA": c(2, 2), "VA": c(1, 2), "VB": c(0, 2)}

    def turn(last):
        n = counts()
        return [
            Slot(("A", od, 1, ("A", ev)), [("OA", ev, 0), ("VA", od, 1), ("F", ev, 0), ("PB", ev, 0)], n),
            Slot(("B", ev, 0, ("A", od)), [("OA", od, 1), ("VB", ev, 0), ("F", od, 1), ("PB", od, 1)], n),
            Slot(("B", od, 1, ("B", ev)), [("OB", ev, 0), ("VB", od, 1), ("F", ev, 0)] + [("PA", ev2, 0)] * (not last), n),
            Slot(None if last else ("A", ev2, 0, ("B", od)),
                 [("OB", od, 1)] + [("VA", ev2, 0)] * (not last) + [("F", od, 1)] + [("PA", od2, 1)] * (not last), n),
        ]

    body, tail = turn(False), turn(True)
    for slots in (body, tail):
        for s, after in zip(slots, slots[1:]):
            s.early = after.out
    first[-1].early = body[0].out
    body[-1].early = Block("OA", ev2, 0, {k: c(v.const + v.per, v.per) for k, v in counts().items()})
    return first, body, tail


def pass_at(s, tick):
    first, tick = FIRST[s.att[0] if s.att else "A"], max(tick, 0)
    return (False, tick, first) if tick < first else (True, tick - first, TICKS - first)


def units_at(u, ticks, count):
    return range(u * count // ticks, (u + 1) * count // ticks)


def batches_due(kind, u):
    for j in range(GROUPS):
        for b, units in enumerate(BATCHES[kind]):
            if min(j * NU[kind] + units[-1] + LAGS[kind][b], UNITS[kind]) == u:
                yield j, b


def out_first(block):
    return GU[block.name] - GROUPS


def spread(ap, n):
    return bass.AP(tensor=ap.tensor, offset=ap.offset, ap=[list(x) for x in ap.ap] + [[0, n]])


def build(nc, x_in, Wq, bq, Wk, bk, Wv, bv, Wo, bo, Wqkv, Wout, bout, w_gate, w_up, w_down,
          cos_in, sin_in, masks_in, eye_in, sel_in, swap_in, strip_in, out):
    nc.disable_value_cache = True
    first, body, tail = schedule()
    ctx = ExitStack()
    with ctx:
        def sb(name, shape, dt):
            return ctx.enter_context(nc.sbuf_tensor(name, shape, dt))

        def sem(name):
            return ctx.enter_context(nc.semaphore(name))

        wa_qk = [sb(f"wa_qk{i}", [P, KT, 2 * D], F32R) for i in range(2)]
        wa_v = [sb(f"wa_v{i}", [P, KT, D], F32R) for i in range(2)]
        wa_o = [sb(f"wa_o{i}", [P, GROUPS, D], F32R) for i in range(2)]
        wb_qk = [sb(f"wb_qk{i}", [P, KT, 2 * D], F32R) for i in range(2)]
        wb_v = [sb(f"wb_v{i}", [P, KT, D], F32R) for i in range(2)]
        wb_o = [sb(f"wb_o{i}", [P, GROUPS, D], F32R) for i in range(2)]
        w_g = sb("w_g", [P, KT, HID], F32R)
        w_u = sb("w_u", [P, KT, HID], F32R)
        w_d = sb("w_d", [P, FT, D], F32R)
        cos = sb("cos", [P, S], F32)
        sin = sb("sin", [P, S], F32)
        mask03 = sb("mask03", [P, WIDTH_A[1]], BF16)
        mask12 = sb("mask12", [P, WIDTH_A[5]], BF16)
        causal = sb("causal", [P, P], BF16)
        eye = sb("eye", [P, P], F32)
        eye_bf = sb("eye_bf", [P, P], BF16)
        swap = sb("swap", [P, P], F16)
        far = sb("far", [P, P + 1 + GLOBALS], BF16)
        glob_mask = far[:, 0:P]
        ones = far[:, P:P + 1]
        glob_sel = far[:, P + 1:]
        own_strip = sb("own_strip", [P, HEADS], F32)
        sel = sb("sel", [2 * HEADS, HEADS], BF16)
        qk_bias = sb("qk_bias", [P, 4], F32)
        v_bias = sb("v_bias", [P, D], F32)
        o_bias = [sb(f"o_bias{i}", [P, D], F32) for i in range(2)]
        eps = sb("eps", [P, NT], F32)
        pause = sb("pause", [1, 1], F32)
        minus_half = sb("minus_half", [P, NT], F32)
        general = sb("general", [1, 1], I32)
        x = [sb(f"x{i}", [P, NT, D], F32) for i in range(2)]
        x_next = sb("x_next", [P, NT, D], F32)
        xn = sb("xn", [P, NT, D], F32)
        xT = [sb(f"xT{i}", [P, KT, S], F32R) for i in range(2)]
        stats = sb("stats", [P, NT, 6], F32)
        mv = sb("mv", [P, NT, 2], F32)
        veps = sb("veps", [P, NT], F32)
        root = sb("root", [P, NT], F32)
        newton = sb("newton", [P, NT], F32)
        w_top, w_top1 = newton[:, 0:1], root[0:1, 0:1]
        src = sb("src", [P, 2, 2, 2, 2, S], F16)
        pack = sb("pack", [P, 2, PACK], F16)
        v_aug = [sb(f"v_aug{i}", [P, NT, HEADS, DH + 1], F32) for i in range(2)]
        v_glob = sb("v_glob", [P, HEADS, DH + 1], F32)
        top = sb("top", [P, NT + 1, HEADS], F32)
        top_glob = sb("top_glob", [P, GROUPS], F32)
        ntop = sb("ntop", [P, NT + 1, 2 * HEADS], BF16)
        ntopT = sb("ntopT", [2 * HEADS, S], BF16)
        probs = sb("probs", [P, RING, S], F32)
        den = [sb(f"den{i}", [P, GROUPS, NT, 4], F32) for i in range(2)]
        rden = sb("rden", [P, GROUPS, NT, 4], F32)
        o_sb = sb("o_sb", [P, GROUPS, S], F32)
        tmp = sb("tmp", [P, 4, S], F32)
        h = [sb(f"h{i}", [P, 2, S], F32R) for i in range(2)]
        s_bank = [ctx.enter_context(nc.psum_tensor(f"s_bank{i}", [P, S], F32)) for i in range(3)]
        o_bank = ctx.enter_context(nc.psum_tensor("o_bank", [P, S], F32))
        gu_bank = [ctx.enter_context(nc.psum_tensor(f"gu_bank{i}", [P, S], F32)) for i in range(2)]
        d_bank = ctx.enter_context(nc.psum_tensor("d_bank", [P, NT, D], F32))

        def d_half(i):
            return d_bank[:, 2 * i:2 * i + 2, :].rearrange("p a b -> p (a b)")


        def q_pack(b):
            return pack[:, b, 0:PAIRS * S].rearrange("p (n s) -> p n s", s=S)

        def k_pack(b):
            return pack[:, b, PAIRS * S:PACK].rearrange("p (n s) -> p n s", s=S)

        BUFFER = {("A", 0): 1, ("A", 1): 0, ("U", 0): 1, ("U", 1): 1, ("R", 0): 0, ("R", 1): 0}

        w_in = sem("w_in")
        c_in = sem("c_in")
        zeroed = sem("zeroed")
        cleared = sem("cleared")
        filled = sem("filled")
        w_f32 = sem("w_f32")
        w_turned = sem("w_turned")
        w_taken = sem("w_taken")
        w_staged = sem("w_staged")
        wb_split = sem("wb_split")
        w_raw = sem("w_raw")
        w_flag = sem("w_flag")
        prep = sem("prep")
        packed = {(k, i, j): sem(f"packed_{k}{i}{j}") for k in "AUR" for i in range(2) for j in range(GROUPS)}
        a1_scores = sem("a1_scores")
        a1_taken = sem("a1_taken")
        v_glob_in = sem("v_glob_in")
        ntop_ready = sem("ntop_ready")
        ntop_turned = sem("ntop_turned")
        ntopT_ready = sem("ntopT_ready")
        top_link = sem("top_link")
        a_scores = sem("a_scores")
        a_exp = sem("a_exp")
        a_used = sem("a_used")
        a_out_taken = sem("a_out_taken")
        den_scores = sem("den_scores")
        den_exp = sem("den_exp")
        b_scores = sem("b_scores")
        b_exp = sem("b_exp")
        b_used = sem("b_used")
        b_out_taken = sem("b_out_taken")
        x_landed = sem("x_landed")
        x_stored = [sem(f"x_stored{i}") for i in range(2)]
        gu_ready = sem("gu_ready")
        gu_taken = sem("gu_taken")
        d_ready = sem("d_ready")
        d_taken = sem("d_taken")
        link = sem("link")
        mv_ready = sem("mv_ready")
        pool_link = sem("pool_link")
        root_ready = sem("root_ready")
        xn_ready = sem("xn_ready")
        xT_high = sem("xT_high")
        biased = sem("biased")
        spread_ready = sem("spread_ready")
        on_high = sem("on_high")
        on_ready = sem("on_ready")
        on_used = sem("on_used")
        tanh_ready = sem("tanh_ready")
        h_high = sem("h_high")
        h_ready = sem("h_ready")
        h_used = sem("h_used")
        qk_high = sem("qk_high")
        rot_sum = sem("rot_sum")
        rot_high = sem("rot_high")
        rot_ready = sem("rot_ready")

        st = pack[:, :, :].rearrange("p b n -> p (b n)").bitcast(F32)
        at = [0]

        def stage(*shape):
            n = int(np.prod(shape))
            a = st[:, at[0]:at[0] + n]
            at[0] += n
            names = "abc"[:len(shape)]
            return a.rearrange(f"p ({' '.join(names)}) -> p {' '.join(names)}", **dict(zip(names, shape)))

        st_qkv = [stage(KT, D) for _ in range(3)]
        st_o = stage(KT, D)
        st_ocols = stage(KT, GROUPS * P)
        st_bqkv = stage(KT, 3 * D)
        st_brows = stage(GROUPS, D)
        st_int = st[:, at[0]:at[0] + 3 * FT * D].bitcast(I32)
        st_f32 = stage(3 * FT * D)
        st_dT = stage(FT, D)
        st2 = src[:, :, :, :, :, :].rearrange("p a b c d s -> p (a b c d s)").bitcast(F32)
        st_gT = st2[:, 0:KT * HID].rearrange("p (k n) -> p k n", k=KT)
        st_uT = st2[:, KT * HID:2 * KT * HID].rearrange("p (k n) -> p k n", k=KT)
        all_banks = [b[:, :] for b in s_bank] + [o_bank[:, :]] + [b[:, :] for b in gu_bank] + \
                    [d_half(0), d_half(1)]
        NW, NC = 12, 16

        block = ctx.enter_context(nc.Block())

        @block.sync
        def _(sp):
            for st_w, w in zip(st_qkv + [st_o], (Wq, Wk, Wv, Wo)):
                sp.dma_start(st_w, w.rearrange("(t p) n -> p t n", p=P)).then_inc(w_in, 16)
            sp.dma_start(st_bqkv, Wqkv.rearrange("(t p) n -> p t n", p=P)).then_inc(w_in, 16)
            for n, w in enumerate((w_gate, w_up, w_down)):
                rows = w.shape[0] // P
                dst = st_int[:, n * FT * D:(n + 1) * FT * D].rearrange("p (t n) -> p t n", t=rows)
                sp.dma_start(dst, w.rearrange("(t p) n -> p t n", p=P)).then_inc(w_in, 16)
            sp.wait_ge(zeroed, 2)
            for c in range(4):
                rows = Wout.rearrange("(t j r d) n -> t r d j n", t=2, j=GROUPS, r=2)[c // 2, c % 2]
                sp.dma_start(st_brows[32 * c:32 * c + DH], rows).then_inc(w_in, 16)
            for dst, a in ((cos, cos_in), (sin, sin_in), (eye, eye_in), (swap, swap_in), (own_strip, strip_in)):
                sp.dma_start(dst[:, :], a).then_inc(c_in, 16)
            col = 0
            for m in (mask03, mask12, causal, eye_bf, far):
                n = m.shape[1]
                sp.dma_start(m[:, :], masks_in[:, col:col + n].bitcast(BF16)).then_inc(c_in, 16)
                col += n
            sp.dma_start(sel[:, :], sel_in.bitcast(BF16)).then_inc(c_in, 16)
            for n, b in enumerate((bq, bk)):
                sp.dma_start(qk_bias[:, 2 * n:2 * n + 2], b.rearrange("(t p) -> p t", p=P),
                             allow_slow_non_contiguous=True).then_inc(c_in, 16)
            for dst, b in ((v_bias, bv), (o_bias[0], bo), (o_bias[1], bout)):
                sp.dma_start(dst[:, :], b.partition_broadcast(P)).then_inc(c_in, 16)
            for n, (dst, a) in enumerate(((w_g, st_gT), (w_u, st_uT), (w_d, st_dT))):
                sp.wait_ge(w_staged, (4, 8, 11)[n])
                sp.dma_start(dst[:, :, :].bitcast(F32), a).then_inc(w_raw, 16)

            def load_q(kind, parity):
                rotated, qp = int(kind == "R"), q_pack(BUFFER[kind, parity])
                for j in range(GROUPS):
                    for n in range(4):
                        sp.dma_start(qp[32 * n:32 * n + 32, 2 * j:2 * j + 2, :], src[32 * j:32 * j + 32, rotated, 0, n // 2, :, :])\
                            .then_inc(packed[kind, parity, j], 16)

            def load_k(kind, parity):
                rotated, kp = int(kind == "R"), k_pack(BUFFER[kind, parity])
                for j in range(GROUPS):
                    for n in range(4):
                        for e in range(2):
                            r = slice(32 * j + DH * e, 32 * j + DH * e + DH)
                            sp.dma_start(kp[32 * n + DH * e:32 * n + DH * e + DH, 4 * j + e:4 * j + e + 3:2, :],
                                         src[r, rotated, 1, n % 2, :, :]).then_inc(packed[kind, parity, j], 16)

            def slot(s, turn):
                if s.proj and s.proj.name == "PA":
                    if s.proj.seq.const:
                        sp.wait_ge(biased, s.proj.p.at(turn))
                    sp.dma_start(x_next[:, :, :],
                                 x_in[bass.ds(s.proj.seq.at(turn), 1)].rearrange("a (t p) n -> p (a t) n", p=P))\
                        .then_inc(x_landed, 16)
                if s.v and s.v.name == "VA":
                    seq, parity = s.v.seq, s.v.parity
                    if not seq.per:
                        sp.wait_ge(filled, 1)
                    sp.wait_ge(d_taken, (s.v.d + 1).at(turn))
                    if seq.const:
                        sp.wait_ge(a_used, (seq * USES).at(turn))
                    for c in range(4):
                        first_head = 8 * (c // 2) + c % 2
                        sp.dma_start(v_glob[32 * c:32 * c + GLOBALS, c::4, :],
                                     v_aug[parity][0:GLOBALS, 0, first_head:first_head + 7:2, :]).then_inc(v_glob_in, 16)
                if s.att and s.att[0] == "B":
                    _, seq, parity, _ = s.att
                    sp.wait_ge(rot_ready, (seq * 4 + 4).at(turn))
                    if parity == 0:
                        sp.wait_ge(a_scores, ((seq + 2) * UNITS["A"]).at(turn))
                    else:
                        sp.wait_ge(b_scores, (seq * UNITS["B"]).at(turn))
                    load_q("R", parity)
                    load_k("R", parity)
                if s.out and s.out.name == "OB":
                    seq, parity = s.ffn.seq, s.ffn.parity
                    sp.wait_ge(d_taken, (s.ffn.d + DU["F"]).at(turn))
                    sp.dma_start(out[bass.ds(seq.at(turn), 1)].rearrange("a (t p) n -> p (a t) n", p=P),
                                 x[parity][:, :, :]).then_inc(x_stored[parity], 16)
                if s.proj:
                    name, seq, parity = s.proj.name, s.proj.seq, s.proj.parity
                    if name == "PB" and parity == 0:
                        sp.wait_ge(a_scores, ((seq + 1) * UNITS["A"]).at(turn))
                    elif name == "PB":
                        sp.wait_ge(den_scores, (seq * DEN_UNITS).at(turn))
                    elif parity == 0 and seq.per:
                        sp.wait_ge(den_scores, (seq * DEN_UNITS).at(turn))
                    elif seq.per:
                        sp.wait_ge(b_scores, ((seq + -1) * UNITS["B"]).at(turn))
                    else:
                        sp.wait_ge(cleared, parity + 1)
                    kind, per = ("U", 2) if name == "PB" else ("A", 1)
                    sp.wait_ge(gu_taken, (s.proj.gu + (per + 1)).at(turn))
                    load_q(kind, parity)
                    sp.wait_ge(gu_taken, (s.proj.gu + (3 * per + 1)).at(turn))
                    load_k(kind, parity)

            for s in first:
                slot(s, 0)
            with sp.Fori(0, SEQS // 2 - 1) as turn:
                for s in body:
                    slot(s, turn)
            for s in tail:
                slot(s, SEQS // 2 - 1)
            for i in range(2):
                sp.wait_ge(x_stored[i], 16 * SEQS // 2)

        @block.tensor
        def _(pe):
            banks = []
            for n in range(3):
                banks.append([(k * D + t * P, st_qkv[n][:, t, k * P:(k + 1) * P]) for k in range(KT) for t in range(KT)])
            for half in range(2):
                banks.append([(j * D + t * P, st_ocols[:, t, (2 * half + j) * P:(2 * half + j + 1) * P])
                              for j in range(2) for t in range(KT)])
            for n in range(2):
                w = st_f32[:, n * FT * D:(n + 1) * FT * D].rearrange("p (t n) -> p t n", t=FT)
                for k in range(KT):
                    for half in range(2):
                        banks.append([(t * P, w[:, 3 * half + t, k * P:(k + 1) * P]) for t in range(3)])
            w = st_f32[:, 2 * FT * D:].rearrange("p (t n) -> p t n", t=KT)
            for pair in range(FT // 2):
                banks.append([(f * D + t * P, w[:, t, (2 * pair + f) * P:(2 * pair + f + 1) * P])
                              for f in range(2) for t in range(KT)])
            pe.wait_ge(c_in, 16 * NC)
            pe.wait_ge(w_in, 16 * NW)
            pe.wait_ge(w_f32, 2)
            for n, bank in enumerate(banks):
                if n >= len(all_banks):
                    last = n - len(all_banks)
                    pe.wait_ge(w_taken if last < 5 else w_staged, last + 1 if last < 5 else last - 4)
                for c0, a in bank:
                    last = pe.transpose(all_banks[n % len(all_banks)][:, c0:c0 + P], a, eye[:, :])
                last.then_inc(w_turned, 1)
            pe.wait_ge(w_taken, 5)
            pe.wait_ge(w_staged, len(banks) - 5)
            pe.wait_ge(w_flag, 1)
            pe.transpose(gu_bank[0][0:1, 0:P], w_top, eye[:, :]).then_inc(w_turned, 1)
            pe.wait_ge(w_flag, 3)
            pe.wait_ge(w_raw, 48)
            is_general = pe.value_load(general[0:1, 0:1], min_val=0, max_val=1)

            def unit_bank(u):
                return s_bank[u % 3]

            def split_passes(lhs, rhs):
                return ((lhs[0], rhs[0]), (lhs[1], rhs[0]), (lhs[0], rhs[1]))

            def outputs_taken(s, turn, j):
                kind, seq, parity, prev = s.att
                if j:
                    pe.wait_ge(a_out_taken if kind == "A" else b_out_taken, (seq * GROUPS + j).at(turn))
                elif prev:
                    kind, pseq = prev
                    pe.wait_ge(a_out_taken if kind == "A" else b_out_taken, ((pseq + 1) * GROUPS).at(turn))

            def value(parity, j, c, t, n):
                return v_aug[parity][:, t, 8 * (c // 2) + 2 * j + c % 2, 0:n]

            def a_unit(s, turn, u, by_key):
                _, seq, parity, prev = s.att
                qp, kp = q_pack(BUFFER["A", parity]), k_pack(BUFFER["A", parity])
                j, n = divmod(u, NU["A"])
                if not by_key and n == 0:
                    per_turn = seq.per // 2
                    pe.wait_ge(packed["A", parity, j],
                               Count(SETDMA * (seq.const // 2 + 1), SETDMA * per_turn).at(turn))
                if not by_key and u == 0 and prev:
                    kind, pseq = prev
                    pe.wait_ge(a_exp if kind == "A" else b_exp, ((pseq + 1) * UNITS[kind]).at(turn))
                if by_key and u == 0:
                    pe.wait_ge(ntopT_ready, (seq + 1).at(turn))
                if u >= 3:
                    pe.wait_ge(a_exp if by_key else a1_taken, (seq * UNITS["A"] + (u - 2)).at(turn))
                bank = unit_bank(u)
                if n == 0:
                    if by_key:
                        pe.matmul(bank[:, :], glob_mask, spread(ones, S)[:, 0, :], start=True, stop=False, skip_group_check=True)
                    for c in range(4):
                        q, k = qp[:, 2 * j + c // 2, :], kp[:, 4 * j + c, :]
                        stat, moving = (k, q) if by_key else (q, k)
                        last = pe.matmul(bank[32 * c:32 * c + 32, :], stat[:, 0:32], moving, start=not by_key, stop=not by_key,
                                         tile_position=(0, 32 * c), skip_group_check=True)
                    for c in range(4 * by_key):
                        last = pe.matmul(bank[32 * c:32 * c + 32, :], spread(sel[:, 4 * j + c], 32), ntopT[:, :],
                                         start=False, stop=True, tile_position=(0, 32 * c), skip_group_check=True)
                else:
                    mask = mask03 if n < 5 else mask12
                    pe.matmul(bank[:, 0:mask.shape[1]], eye_bf[:, :], mask[:, :], start=True, stop=False, skip_group_check=True)
                for c, t, c0 in UNITS_A[n]:
                    hh, pair = 4 * j + c, 2 * j + c // 2
                    stat = (kp[:, hh, :] if by_key else qp[:, pair, :])[:, t * P:(t + 1) * P]
                    moving = qp[:, pair, :] if by_key else kp[:, hh, :]
                    a, b = WINDOW[t]
                    pieces = [(c0, a, b)] + ([(c0 + b - a, 0, GLOBALS)] if t else [])
                    for col, a, b in pieces:
                        last = pe.matmul(bank[:, col:col + b - a], stat, moving[:, a:b], start=False, stop=not by_key,
                                         skip_group_check=True)
                    for col, a, b in pieces * by_key:
                        last = pe.matmul(bank[:, col:col + b - a], spread(sel[:, hh], P), ntopT[:, a:b],
                                         start=False, stop=True, skip_group_check=True)
                last.then_inc(a_scores if by_key else a1_scores, 1)

            def a_values(s, turn, j, batch):
                _, seq, parity, _ = s.att
                units = BATCHES["A"][batch]
                if batch == 0:
                    outputs_taken(s, turn, j)
                    if j == 0:
                        pe.wait_ge(v_glob_in, ((seq + 1) * 64).at(turn))
                pe.wait_ge(a_exp, (seq * UNITS["A"] + (j * NU["A"] + units[-1] + 1)).at(turn))
                pieces = [(-1, 0, c, 0, 0, 0, S) for c in range(4)] if batch == 0 else []
                for n in units:
                    for c, t, c0 in UNITS_A[n]:
                        a, b = WINDOW[t]
                        pieces.append((t, 0, c, n, c0, a, b))
                        if t:
                            pieces.append((t, 1, c, n, c0 + b - a, 0, GLOBALS))
                for t, _, c, n, col, a, b in sorted(pieces):
                    v = v_glob[:, 4 * j + c, :] if batch == 0 else value(parity, j, c, t, DH + 1)
                    last = pe.matmul(o_bank[32 * c:32 * c + DH + 1, a:b], v, probs[:, (j * NU["A"] + n) % RING, col:col + b - a],
                                     start=batch == 0, stop=t == 2, tile_position=(0, 32 * c), skip_group_check=True)
                last.then_inc(a_used, 1)

            def turn_maxima(s, turn):
                _, seq, parity, _ = s.att
                pe.wait_ge(ntop_ready, (seq + 1).at(turn))
                bank = unit_bank(0)[0:2 * HEADS, :]
                pe.matmul(bank[:, 0:GLOBALS], ntop[:, NT, :], glob_sel, start=True, stop=True, skip_group_check=True)
                for t in range(NT):
                    a = GLOBALS if t == 0 else 0
                    last = pe.matmul(bank[:, t * P + a:(t + 1) * P], ntop[:, t, :], eye_bf[:, a:], start=True, stop=True,
                                     skip_group_check=True)
                last.then_inc(ntop_turned, 1)

            def den_unit(s, turn, u):
                _, seq, parity, prev = s.att
                qp, kp = q_pack(BUFFER["U", parity]), k_pack(BUFFER["U", parity])
                hh, t = divmod(u, NT)
                if u % (4 * NT) == 0:
                    pe.wait_ge(packed["U", parity, hh // 4], Count(SETDMA, SETDMA).at(turn))
                if u == 0:
                    kind, pseq = prev
                    pe.wait_ge(a_exp if kind == "A" else b_exp, ((pseq + 1) * UNITS[kind]).at(turn))
                if u >= 3:
                    pe.wait_ge(den_exp, (seq * DEN_UNITS + (u - 2)).at(turn))
                pe.matmul(unit_bank(u)[:, :], qp[:, hh // 2, t * P:(t + 1) * P], kp[:, hh, :],
                          start=True, stop=True).then_inc(den_scores, 1)

            def b_unit(s, turn, u):
                _, seq, parity, _ = s.att
                qp, kp = q_pack(BUFFER["R", parity]), k_pack(BUFFER["R", parity])
                j, n = divmod(u, NU["B"])
                if n == 0:
                    pe.wait_ge(packed["R", parity, j], Count(SETDMA, SETDMA).at(turn))
                if u == 0:
                    pe.wait_ge(den_exp, ((seq + 1) * DEN_UNITS).at(turn))
                if u >= 3:
                    pe.wait_ge(b_exp, (seq * UNITS["B"] + (u - 2)).at(turn))
                bank = unit_bank(u)
                for i, (c, t, c0) in enumerate(UNITS_B[n]):
                    pe.matmul(bank[:, c0:c0 + P], eye_bf[:, :], causal[:, :], start=i == 0, stop=False,
                              skip_group_check=True)
                for c, t, c0 in UNITS_B[n]:
                    last = pe.matmul(bank[:, c0:c0 + S - t * P], kp[:, 4 * j + c, t * P:(t + 1) * P],
                                     qp[:, 2 * j + c // 2, t * P:S], start=False, stop=True, skip_group_check=True)
                last.then_inc(b_scores, 1)

            def b_values(s, turn, j, batch):
                _, seq, parity, _ = s.att
                if batch == 0:
                    outputs_taken(s, turn, j)
                pe.wait_ge(b_exp, (seq * UNITS["B"] + (j * NU["B"] + BATCHES["B"][batch][-1] + 1)).at(turn))
                pieces = [(t, c, n, c0) for n in BATCHES["B"][batch] for c, t, c0 in UNITS_B[n]]
                for t, c, n, c0 in sorted(pieces):
                    last = pe.matmul(o_bank[32 * c:32 * c + DH, t * P:S], value(parity, j, c, t, DH),
                                     probs[:, (j * NU["B"] + n) % RING, c0:c0 + S - t * P], start=t == 0, stop=t == 2,
                                     tile_position=(0, 32 * c), skip_group_check=True)
                last.then_inc(b_used, 1)

            def gu(block, k, turn):
                if (block.gu + (k - 1)).const > 0:
                    pe.wait_ge(gu_taken, (block.gu + (k - 1)).at(turn))
                return gu_bank[k % 2]

            def sums(block, n, turn):
                pe.wait_ge(a_out_taken, (block.seq * GROUPS + 2 * (n + 1)).at(turn))
                if n == 0:
                    pe.wait_ge(d_taken, block.d.at(turn))
                    banks = [d_half(0), d_half(1)]
                else:
                    banks = [gu(block, k, turn)[:, :] for k in range(2)]
                for jj in range(2):
                    for t in range(NT):
                        last = pe.transpose(banks[jj][:, t * P:(t + 1) * P], o_sb[:, 2 * n + jj, t * P:(t + 1) * P], eye[:, :])
                    if n or jj:
                        last.then_inc(gu_ready if n else d_ready, 1)

            def out_step(block, n, turn):
                w = wa_o if block.name == "OA" else wb_o
                if n < GROUPS:
                    bank = gu(block, out_first(block) + n, turn)
                    pe.wait_ge(spread_ready, (block.o * GROUPS + (n + 1)).at(turn))
                    for t in range(NT):
                        last = pe.transpose(bank[:, t * P:(t + 1) * P], tmp[:, n, t * P:(t + 1) * P], eye[:, :])
                    last.then_inc(gu_ready, 1)
                if n >= 2:
                    j = n - 2
                    if j == 0:
                        pe.wait_ge(d_taken, (block.d + (DU[block.name] - 2)).at(turn))
                    pe.wait_ge(on_ready, (block.o * GROUPS + (j + 1)).at(turn))
                    for t in range(NT):
                        for i, (a, b) in enumerate(split_passes(h, w)):
                            last = pe.matmul(d_bank[:, t, :], a[:, j % 2, t * P:(t + 1) * P], b[:, j, :],
                                             start=j == 0 and i == 0 and t % 2 == 0, stop=j == GROUPS - 1 and i == 2,
                                             skip_group_check=True)
                        if j == GROUPS - 1 and t % 2:
                            last.then_inc(d_ready, 1)
                    if j < GROUPS - 1:
                        last.then_inc(on_used, 1)

            def turn_x(block, turn):
                banks = [d_half(k) for k in range(KT)]
                if block.d.const:
                    pe.wait_ge(d_taken, block.d.at(turn))
                for t in range(NT):
                    pe.wait_ge(xn_ready, (block.ln * NT + (t + 1)).at(turn))
                    for k in range(KT):
                        last = pe.transpose(banks[k][:, t * P:(t + 1) * P], xn[:, t, k * P:(k + 1) * P], eye[:, :])
                        if t == NT - 1:
                            last.then_inc(d_ready, 1)

            def plain(a, exact):
                return a if exact else a.bitcast(F32)

            def x_there(block, part, k, turn):
                if part:
                    pe.wait_ge(d_taken, (block.d + (k + 1)).at(turn))
                else:
                    pe.wait_ge(xT_high, (block.ln * KT + (k + 1)).at(turn))

            def ffn_up(block, f, up, part, turn, exact):
                w = w_u if up else w_g
                if part == 0:
                    gu(block, 2 * f + up, turn)
                for k in range(KT):
                    if f == 0 and not up:
                        x_there(block, part, k, turn)
                    last = pe.matmul(gu_bank[up][:, :], plain(w[:, k, f * P:(f + 1) * P], exact), plain(xT[part][:, k, :], exact),
                                     start=k == 0 and part == 0, stop=k == KT - 1 and part == 1)
                if part:
                    last.then_inc(gu_ready, 1)

            def ffn_down(block, f, turn, exact):
                if f == 0:
                    pe.wait_ge(d_taken, (block.d + KT).at(turn))
                pe.wait_ge(h_ready, (block.f * FT + (f + 1)).at(turn))
                for t in range(NT):
                    for i in range(2):
                        last = pe.matmul(d_bank[:, t, :], plain(h[i][:, f % 2, t * P:(t + 1) * P], exact),
                                         plain(w_d[:, f, :], exact), start=f == 0 and i == 0 and t % 2 == 0,
                                         stop=f == FT - 1 and i == 1, skip_group_check=True)
                    if f == FT - 1 and t % 2:
                        last.then_inc(d_ready, 1)
                if f < FT - 1:
                    last.then_inc(h_used, 1)

            def qk_step(block, n, turn):
                pa = block.name == "PA"
                bank = gu(block, n if pa else 2 * n, turn)
                w = wa_qk if pa else wb_qk
                for i, (part, w_part) in enumerate(((0, w[0]), (0, w[1]), (1, w[0]))):
                    for k in range(KT):
                        if n == 0 and i != 1:
                            x_there(block, part, k, turn)
                        last = pe.matmul(bank[:, :], w_part[:, k, n * P:(n + 1) * P], xT[part][:, k, :],
                                         start=k == 0 and i == 0, stop=k == KT - 1 and i == 2)
                last.then_inc(gu_ready, 1)

            def swap_step(block, n, turn):
                pe.wait_ge(gu_taken, (block.gu + (2 * n + 1)).at(turn))
                for i in range(2):
                    last = pe.matmul(gu_bank[1][:, :], swap[:, :], src[:, 0, n // 2, i, n % 2, :], start=i == 0, stop=i == 1)
                last.then_inc(gu_ready, 1)

            def v_step(block, turn):
                w = wa_v if block.name == "VA" else wb_v
                if block.d.const:
                    pe.wait_ge(d_taken, block.d.at(turn))
                for t in range(NT):
                    for k in range(KT):
                        for i, (a, b) in enumerate(split_passes(xT, w)):
                            last = pe.matmul(d_bank[:, t, :], a[:, k, t * P:(t + 1) * P], b[:, k, :],
                                             start=k == 0 and i == 0 and t % 2 == 0, stop=k == KT - 1 and i == 2,
                                             skip_group_check=True)
                last.then_inc(d_ready, 1)

            def slot(s, turn, exact):
                values = {"A": a_values, "B": b_values}
                for tick in range(-1, TICKS):
                    second, u, ticks = pass_at(s, tick)
                    if s.att and tick >= 0:
                        kind = s.att[0]
                        if kind == "A" and second and u == 0:
                            turn_maxima(s, turn)
                        count = DEN_UNITS if kind == "B" and not second else UNITS[kind]
                        for i in units_at(u, ticks, count):
                            if kind == "A":
                                a_unit(s, turn, i, second)
                            else:
                                (b_unit if second else den_unit)(s, turn, i)
                            for j, b in batches_due(kind, i) if second else ():
                                values[kind](s, turn, j, b)
                    for kind, n, block in s.steps(tick):
                        if kind == "S" and block.name == "OA":
                            sums(block, n, turn)
                        elif kind == "O":
                            out_step(block, n, turn)
                        elif kind == "X":
                            turn_x(block, turn)
                        elif kind == "G" and n == 0:
                            for up, part in ((0, 0), (1, 0), (0, 1)):
                                ffn_up(block, n, up, part, turn, exact)
                        elif kind in "GU":
                            for part in range(int(kind == "U" and n == 0), 2):
                                ffn_up(block, n, int(kind == "U"), part, turn, exact)
                        elif kind == "D":
                            ffn_down(block, n, turn, exact)
                        elif kind == "T":
                            qk_step(block, n, turn)
                        elif kind == "W":
                            swap_step(block, n, turn)
                        elif kind == "V":
                            v_step(block, turn)
                if s.att:
                    for j, b in batches_due(s.att[0], UNITS[s.att[0]]):
                        values[s.att[0]](s, turn, j, b)

            def slots(exact):
                for s in first:
                    slot(s, 0, exact)
                with pe.Fori(0, SEQS // 2 - 1) as turn:
                    for s in body:
                        slot(s, turn, exact)
                for s in tail:
                    slot(s, SEQS // 2 - 1, exact)

            with pe.If(is_general > 0):
                slots(False)
            with pe.Else():
                slots(True)

        @block.scalar
        def _(act):
            def exp(s, turn, u):
                kind, seq, parity, prev = s.att
                scores, done, used = (a_scores, a_exp, a_used) if kind == "A" else (b_scores, b_exp, b_used)
                n = u % NU[kind]
                width = WIDTH_A[n] if kind == "A" else S
                if u == 0 and prev:
                    pkind, pseq = prev
                    act.wait_ge(a_used if pkind == "A" else b_used, ((pseq + 1) * USES).at(turn))
                act.wait_ge(scores, (seq * UNITS[kind] + (u + 1)).at(turn))
                if u >= RING:
                    pj, pn = divmod(u - RING, NU[kind])
                    act.wait_ge(used, (seq * USES + (pj * 3 + BATCH_OF[kind][pn] + 1)).at(turn))
                act.activation(probs[:, u % RING, 0:width], s_bank[u % 3][:, 0:width], ACT.Exp, scale=SM_SCALE)\
                    .then_inc(done, 1)

            def den_exponential(s, turn, u):
                _, seq, parity, _ = s.att
                hh, t = divmod(u, NT)
                act.wait_ge(den_scores, (seq * DEN_UNITS + (u + 1)).at(turn))
                act.activation(probs[:, u % 3, 0:S // 2].bitcast(BF16), s_bank[u % 3][:, :], ACT.Exp, scale=SM_SCALE,
                               accum_out=den[parity][:, hh // 4, t, hh % 4:hh % 4 + 1]).then_inc(den_exp, 1)

            def x_high(block, turn):
                for k in range(KT):
                    act.wait_ge(d_ready, (block.d + (k + 1)).at(turn))
                    act.activation(xT[0][:, k, :], d_half(k), ACT.Copy).then_inc(xT_high, 1)

            def half_tanh(block, f, turn):
                if f >= 2:
                    act.wait_ge(h_ready, (block.f * FT + (f - 1)).at(turn))
                act.wait_ge(gu_ready, (block.gu + (2 * f + 1)).at(turn))
                act.activation(tmp[:, f % 2, :], gu_bank[0][:, :], ACT.Tanh, scale=0.5 * DEQUANT).then_inc(tanh_ready, 1)

            def qk_step(block, n, att, turn):
                pa = block.name == "PA"
                k = n if pa else 2 * n
                act.wait_ge(gu_ready, (block.gu + (k + 1)).at(turn))
                dst = src[:, 0, n // 2, 0, n % 2, :]
                if pa:
                    act.activation(dst, gu_bank[k % 2][:, :], ACT.Identity, bias=qk_bias[:, n:n + 1]).then_inc(qk_high, 1)
                else:
                    act.activation(dst, gu_bank[k % 2][:, :], ACT.Copy).then_inc(qk_high, 1)

            def rot_high_step(block, n, att, turn):
                if n == 0 and att[0] == "B":
                    for j in range(GROUPS):
                        act.wait_ge(packed["R", att[2], j], Count(SETDMA, SETDMA).at(turn))
                act.wait_ge(rot_sum, (block.seq * 4 + (n + 1)).at(turn))
                act.activation(src[:, 1, n // 2, 0, n % 2, :], tmp[:, 2 * (n % 2), :], ACT.Copy).then_inc(rot_high, 1)

            def slot(s, turn):
                for tick in range(-1, TICKS):
                    second, u, ticks = pass_at(s, tick)
                    if s.att and second:
                        if s.att[0] == "A" and u == 0:
                            act.wait_ge(ntop_turned, (s.att[1] + 1).at(turn))
                            act.activation(ntopT[:, :], s_bank[0][0:2 * HEADS, :], ACT.Copy).then_inc(ntopT_ready, 1)
                        for i in units_at(u, ticks, UNITS[s.att[0]]):
                            exp(s, turn, i)
                    elif s.att and s.att[0] == "B" and tick >= 0:
                        for d in units_at(u, ticks, DEN_UNITS):
                            den_exponential(s, turn, d)
                    for kind, n, block in s.steps(tick):
                        if kind == "X":
                            x_high(block, turn)
                        elif kind == "U":
                            half_tanh(block, n, turn)
                        elif kind == "T1":
                            qk_step(block, n, s.att, turn)
                        elif kind == "W2":
                            rot_high_step(block, n, s.att, turn)

            for n in range(5, 16):
                act.wait_ge(w_turned, n + 1)
                bank = all_banks[n % len(all_banks)]
                if n < 13:
                    dst, k, half = (st_gT, st_uT)[(n - 5) // 4], (n - 5) // 2 % 2, (n - 5) % 2
                    act.activation(dst[:, k, half * 3 * P:(half + 1) * 3 * P], bank[:, 0:3 * P], ACT.Copy).then_inc(w_staged, 1)
                else:
                    f = 2 * (n - 13)
                    act.activation(st_dT[:, f:f + 2, :], bank.rearrange("p (k n) -> p k n", k=2), ACT.Copy).then_inc(w_staged, 1)
            act.wait_ge(c_in, 16 * NC)
            act.wait_ge(w_raw, 48)
            for s in first:
                slot(s, 0)
            with act.Fori(0, SEQS // 2 - 1) as turn:
                for s in body:
                    slot(s, turn)
            for s in tail:
                slot(s, SEQS // 2 - 1)

        @block.vector
        def _(dve):
            done = [0]

            def then(ins):
                done[0] += 1
                ins.then_inc(prep, 1)
                dve.wait_ge(prep, done[0])

            def split(parts, a):
                then(dve.tensor_copy(parts[0], a))
                return dve.tensor_tensor(parts[1], a, parts[0].bitcast(F32), ALU.subtract)

            dve.memset(st_ocols, 0.0).then_inc(zeroed, 1)
            dve.memset(st_brows, 0.0).then_inc(zeroed, 1)
            dve.wait_ge(zeroed, 2)
            dve.wait_ge(w_in, 16 * NW)
            for t in range(KT):
                for c in range(2):
                    dst = st_ocols[:, t, :].rearrange("p (j a r d) -> p j a r d", j=GROUPS, a=2, r=2)[:, :, c, :, 0:DH]
                    a = st_o[:, t, :].rearrange("p (a j r d) -> p a j r d", a=2, j=GROUPS, r=2)[:, c, :, :, :]
                    last = dve.tensor_copy(dst, a)
            last.then_inc(w_f32, 1)
            dve.tensor_copy(st_f32, st_int).then_inc(w_f32, 1)
            dve.wait_ge(w_f32, 2)
            dve.tensor_reduce(w_top, st_f32, axis=AX.X, op=ALU.max, apply_absolute_value=True).then_inc(w_flag, 1)
            for n in range(5):
                dve.wait_ge(w_turned, n + 1)
                bank = all_banks[n % len(all_banks)]
                if n < 3:
                    w, c = ((wa_qk, 0), (wa_qk, D), (wa_v, 0))[n]
                    split([a[:, :, c:c + D] for a in w], bank.rearrange("p (k n) -> p k n", k=KT)).then_inc(w_taken, 1)
                else:
                    j = 2 * (n - 3)
                    split([a[:, j:j + 2, :] for a in wa_o], bank.rearrange("p (k n) -> p k n", k=2)).then_inc(w_taken, 1)
            dve.wait_ge(w_turned, 17)
            dve.tensor_reduce(w_top1, gu_bank[0][0:1, 0:P], axis=AX.X, op=ALU.max).then_inc(w_flag, 1)
            dve.wait_ge(w_flag, 2)
            dve.tensor_single_scalar(general[:, :], w_top1, EXACT, ALU.is_gt).then_inc(w_flag, 1)
            dve.memset(o_bank[:, :], 0.0)

            def split_b():
                split([w[:, :, :] for w in wb_qk], st_bqkv[:, :, 0:2 * D])
                split([w[:, :, :] for w in wb_v], st_bqkv[:, :, 2 * D:3 * D])
                split([w[:, :, :] for w in wb_o], st_brows).then_inc(wb_split, 1)

            def a_maxima(s, turn, u):
                _, seq, parity, _ = s.att
                j, n = divmod(u, NU["A"])
                bank, hh = s_bank[u % 3], 4 * j + (n - 1) % 4
                if n == 0:
                    dst, a = top_glob[:, j:j + 1], bank[:, :]
                else:
                    dst = top[:, 0:NT:NT - 1, hh] if n < 5 else top[:, 1:3, hh]
                    a = bank[:, 0:WIDTH_A[n]].rearrange("p (a b) -> p a b", a=2)
                dve.wait_ge(a1_scores, (seq * UNITS["A"] + (u + 1)).at(turn))
                dve.reduce_max(dst, a, AX.X).then_inc(a1_taken, 1)

            def minus_maxima(s, turn):
                _, seq, parity, _ = s.att
                dve.wait_ge(a1_taken, ((seq + 1) * UNITS["A"]).at(turn))
                by_strip = [x.rearrange("p (j c) -> p j c", c=4) for x in (top[:, NT, :], own_strip[:, :])]
                dve.tensor_tensor(by_strip[0], spread(top_glob[:, :], 4), by_strip[1], ALU.mult).then_inc(top_link, 1)
                dve.wait_ge(top_link, (seq * 2 + 1).at(turn))
                dve.tensor_scalar(ntop[:, :, 0:HEADS], top[:, :, :], -1.0, None, ALU.mult).then_inc(top_link, 1)
                dve.wait_ge(top_link, (seq * 2 + 2).at(turn))
                dve.scalar_tensor_tensor(ntop[:, :, HEADS:2 * HEADS], top[:, :, :], -1.0, ntop[:, :, 0:HEADS],
                                         ALU.mult, ALU.subtract).then_inc(ntop_ready, 1)

            def take_out(s, turn, j):
                kind, seq, parity, _ = s.att
                used, taken = (a_used, a_out_taken) if kind == "A" else (b_used, b_out_taken)
                dve.wait_ge(used, (seq * USES + (j + 1) * 3).at(turn))
                dve.tensor_copy(o_sb[:, j, :], o_bank[:, :]).then_inc(taken, 1)

            def linked(block, n, ins, turn):
                ins.then_inc(link, 1)
                dve.wait_ge(link, (block.link + n).at(turn))

            def spread_group(block, j, turn):
                dst = tmp[:, j, :].rearrange("p (a b) -> p a b", b=32)
                if j % 2 == 0 and block.pb.const:
                    dve.wait_ge(rot_ready, (block.pb * 4 + (j // 2 - 1)).at(turn))
                dve.tensor_copy(dst, spread(rden[:, j, :, :].rearrange("p t c -> p (t c)"), 32)).then_inc(spread_ready, 1)

            def reciprocals(block, n, turn):
                if block.name == "OA":
                    for jj in range(2):
                        if n == 0:
                            dve.wait_ge(d_ready, (block.d + 1).at(turn))
                            bank = d_half(jj)
                        else:
                            dve.wait_ge(gu_ready, (block.gu + (jj + 1)).at(turn))
                            bank = gu_bank[jj][:, :]
                        a = bank.rearrange("p (t c r) -> p t c r", c=4, r=2 * DH)[:, :, :, DH]
                        ins = dve.reciprocal(rden[:, 2 * n + jj, :, :], a)
                        if n or jj:
                            ins.then_inc(gu_taken if n else d_taken, 1)
                    if not n:
                        dve.wait_ge(d_taken, (block.d + 1).at(turn))
                    else:
                        dve.wait_ge(gu_taken, (block.gu + 2).at(turn))
                elif n == 0:
                    dve.wait_ge(den_exp, ((block.seq + 1) * DEN_UNITS).at(turn))
                    linked(block, 1, dve.reciprocal(rden[:, :, :, :].rearrange("p j t c -> p (j t c)"),
                                                    den[block.parity][:, :, :, :].rearrange("p j t c -> p (j t c)")), turn)
            def out_step(block, n, turn):
                if n < GROUPS:
                    dve.wait_ge(gu_ready, (block.gu + (out_first(block) + n + 1)).at(turn))
                    dve.tensor_tensor(o_sb[:, n, :], o_sb[:, n, :], gu_bank[n % 2][:, :], ALU.mult).then_inc(gu_taken, 1)
                elif n == GROUPS + 1:
                    dve.wait_ge(biased, block.p.at(turn))
                    for t in (0, 2):
                        xs = x[block.parity][:, t:t + 2, :]
                        dve.wait_ge(d_ready, (block.d + (DU[block.name] - 1 + t // 2)).at(turn))
                        dve.tensor_tensor(xs, xs, d_bank[:, t:t + 2, :], ALU.add).then_inc(d_taken, 1)

            def on_high_step(block, n, turn):
                dve.wait_ge(gu_taken, (block.gu + (out_first(block) + n + 1)).at(turn))
                if n >= 2:
                    dve.wait_ge(on_used, (block.o * (GROUPS - 1) + (n - 1)).at(turn))
                dve.tensor_copy(h[0][:, n % 2, :], o_sb[:, n, :]).then_inc(on_high, 1)

            def on_low_step(block, n, turn):
                dve.wait_ge(on_high, (block.o * GROUPS + (n + 1)).at(turn))
                dve.tensor_tensor(h[1][:, n % 2, :], o_sb[:, n, :], h[0][:, n % 2, :].bitcast(F32), ALU.subtract).then_inc(on_ready, 1)

            def normalise(block, part, last, turn):
                xs = x_next if block.name == "PA" else x[block.parity]
                if part:
                    done = (0, 1, 0, 2, 3, 4)[part]
                    if done:
                        dve.wait_ge(link, (block.link + done).at(turn))
                if part == 0:
                    if block.name == "PA":
                        dve.wait_ge(x_landed, ((block.seq + 1) * 16).at(turn))
                    for t in range(NT):
                        if block.name != "PA" and t % 2 == 0:
                            dve.wait_ge(d_taken, (last.d + (DU[last.name] - 1 + t // 2)).at(turn))
                        ins = dve.bn_stats(stats[:, t, :], xs[:, t, :])
                    ins.then_inc(link, 1)
                elif part == 1:
                    dve.memset(pause[:, :], 0.0)
                    for t in range(NT):
                        ins = dve.bn_aggr(mv[:, t, :], stats[:, t, :])
                    ins.then_inc(mv_ready, 1)
                elif part == 2:
                    dve.wait_ge(root_ready, (block.ln + 1).at(turn))
                    dve.scalar_tensor_tensor(newton[:, :], root[:, :], -0.5, root[:, :], ALU.mult, ALU.mult).then_inc(link, 1)
                elif part == 3:
                    dve.tensor_tensor(newton[:, :], newton[:, :], veps[:, :], ALU.mult).then_inc(link, 1)
                elif part == 4:
                    dve.scalar_tensor_tensor(root[:, :], newton[:, :], 1.5, root[:, :], ALU.add, ALU.mult).then_inc(link, 1)
                else:
                    for t in range(NT):
                        dve.tensor_scalar(xn[:, t, :], xs[:, t, :], mv[:, t, 0:1], root[:, t:t + 1], ALU.subtract, ALU.mult)\
                            .then_inc(xn_ready, 1)

            def x_low(block, turn):
                for k in range(KT):
                    dve.wait_ge(xT_high, (block.ln * KT + (k + 1)).at(turn))
                    dve.tensor_tensor(xT[1][:, k, :], d_half(k), xT[0][:, k, :].bitcast(F32), ALU.subtract)\
                        .then_inc(d_taken, 1)

            def gated(block, f, turn):
                t = tmp[:, f % 2, :]
                dve.wait_ge(tanh_ready, (block.f * FT + (f + 1)).at(turn))
                dve.scalar_tensor_tensor(t, t, 1.0, gu_bank[0][:, :], ALU.add, ALU.mult).then_inc(gu_taken, 1)

            def hidden(block, f, turn):
                t = tmp[:, f % 2, :]
                k = block.gu + (2 * f + 1)
                dve.wait_ge(gu_taken, k.at(turn))
                dve.wait_ge(gu_ready, (k + 1).at(turn))
                dve.tensor_tensor(t, t, gu_bank[1][:, :], ALU.mult).then_inc(gu_taken, 1)

            def high(block, f, turn):
                dve.wait_ge(gu_taken, (block.gu + (2 * f + 2)).at(turn))
                if f >= 2:
                    dve.wait_ge(h_used, (block.f * (FT - 1) + (f - 1)).at(turn))
                dve.tensor_copy(h[0][:, f % 2, :], tmp[:, f % 2, :]).then_inc(h_high, 1)

            def add_ffn(block, turn):
                for t in (0, 2):
                    xs = x[block.parity][:, t:t + 2, :]
                    dve.wait_ge(d_ready, (block.d + (KT + 1 + t // 2)).at(turn))
                    dve.scalar_tensor_tensor(xs, d_bank[:, t:t + 2, :], 0.5 * DEQUANT ** 3, xs, ALU.mult, ALU.add)\
                        .then_inc(d_taken, 1)

            def qk_step(block, n, turn):
                pa = block.name == "PA"
                k = n if pa else 2 * n
                dve.wait_ge(qk_high, (block.p * 4 + (n + 1)).at(turn))
                hi, lo = src[:, 0, n // 2, 0, n % 2, :], src[:, 0, n // 2, 1, n % 2, :]
                if pa:
                    dve.scalar_tensor_tensor(lo, gu_bank[k % 2][:, :], qk_bias[:, n:n + 1], hi, ALU.add, ALU.subtract)\
                        .then_inc(gu_taken, 1)
                else:
                    dve.tensor_tensor(lo, gu_bank[0][:, :], hi, ALU.subtract)
                    if n >= 2:
                        dve.wait_ge(rot_ready, (block.seq * 4 + (n - 1)).at(turn))
                    dve.tensor_tensor(tmp[:, 2 * (n % 2), :], gu_bank[0][:, :], cos[:, :], ALU.mult).then_inc(gu_taken, 1)

            def swap_step(block, n, turn):
                dve.wait_ge(gu_ready, (block.gu + (2 * n + 2)).at(turn))
                dve.tensor_tensor(tmp[:, 2 * (n % 2) + 1, :], gu_bank[1][:, :], sin[:, :], ALU.mult).then_inc(gu_taken, 1)

            def v_step(block, turn):
                dve.wait_ge(d_ready, (block.d + 1).at(turn))
                if not block.seq.per:
                    dve.wait_ge(filled, 1)
                for t in range(NT):
                    dst = v_aug[block.parity][:, t, :, 0:DH]
                    a = d_bank[:, t, :].rearrange("p (h d) -> p h d", h=HEADS)
                    if block.name == "VA":
                        ins = dve.tensor_tensor(dst, a, v_bias[:, :].rearrange("p (h d) -> p h d", h=HEADS), ALU.add)
                    else:
                        ins = dve.tensor_copy(dst, a)
                ins.then_inc(d_taken, 1)

            def slot(s, turn):
                for tick in range(-1, TICKS):
                    second, u, ticks = pass_at(s, tick)
                    if s.att and s.att[0] == "A" and not second and tick >= 0:
                        for i in units_at(u, ticks, UNITS["A"]):
                            a_maxima(s, turn, i)
                        if u == ticks - 1:
                            minus_maxima(s, turn)
                    for i in units_at(u, ticks, UNITS[s.att[0]]) if s.att and second else ():
                        for j, b in batches_due(s.att[0], i):
                            if b == 2:
                                take_out(s, turn, j)
                    for kind, n, block in s.steps(tick):
                        if kind == "S1":
                            reciprocals(block, n, turn)
                        elif kind == "S2":
                            for j in (2 * n, 2 * n + 1):
                                spread_group(block, j, turn)
                        elif kind == "O1":
                            out_step(block, n, turn)
                            if n < GROUPS:
                                on_high_step(block, n, turn)
                        elif kind == "O2" and n < GROUPS:
                            on_low_step(block, n, turn)
                        elif kind[0] == "N":
                            normalise(block, int(kind[1]), s.ffn if n else s.out, turn)
                        elif kind == "X1":
                            x_low(block, turn)
                        elif kind == "H":
                            gated(block, n, turn)
                        elif kind == "I":
                            hidden(block, n, turn)
                        elif kind == "J":
                            high(block, n, turn)
                        elif kind == "D" and n == FT - 1:
                            add_ffn(block, turn)
                        elif kind == "T2":
                            qk_step(block, n, turn)
                        elif kind == "W1":
                            swap_step(block, n, turn)
                        elif kind == "V1":
                            v_step(block, turn)
                if s.att:
                    take_out(s, turn, GROUPS - 1)

            slot(first[0], 0)
            split_b()
            slot(first[1], 0)
            with dve.Fori(0, SEQS // 2 - 1) as turn:
                for s in body:
                    slot(s, turn)
            for s in tail:
                slot(s, SEQS // 2 - 1)

        @block.gpsimd
        def _(pool):
            pool.memset(minus_half[:, :], -0.5).then_inc(pool_link, 1)
            pool.memset(eps[:, :], EPS).then_inc(pool_link, 1)
            for i in range(2):
                pool.memset(v_aug[i][:, :, :, :], 1.0)
            pool.memset(v_glob[:, :, :], 0.0).then_inc(filled, 1)
            pool.wait_ge(pool_link, 2)
            pool.wait_ge(c_in, 16 * NC)
            pool.wait_ge(w_raw, 48)
            pool.memset(k_pack(1).rearrange("p n s -> p (n s)").bitcast(F32), 0.0).then_inc(cleared, 1)

            def rsqrt(block, turn):
                pool.wait_ge(mv_ready, (block.ln + 1).at(turn))
                pool.tensor_tensor(veps[:, :], mv[:, :, 1], eps[:, :], ALU.add).then_inc(pool_link, 1)
                pool.wait_ge(pool_link, (block.ln + 3).at(turn))
                pool.tensor_tensor(root[:, :], veps[:, :], minus_half[:, :], ALU.pow).then_inc(root_ready, 1)

            def add_bias(block, turn):
                pool.wait_ge(xn_ready, ((block.ln + 1) * NT).at(turn))
                xs = x[block.parity]
                given = x_next if block.name == "PA" else xs
                if block.name == "PA" and block.seq.per:
                    pool.wait_ge(x_stored[block.parity], Count(16 * (block.seq.const // 2), 16 * (block.seq.per // 2)).at(turn))
                for t in range(NT):
                    ins = pool.tensor_tensor(xs[:, t, :], given[:, t, :], o_bias[block.name == "PB"][:, :], ALU.add)
                ins.then_inc(biased, 1)

            def ffn_step(block, f, turn):
                pool.wait_ge(h_high, (block.f * FT + (f + 1)).at(turn))
                pool.tensor_tensor(h[1][:, f % 2, :], tmp[:, f % 2, :], h[0][:, f % 2, :].bitcast(F32), ALU.subtract)\
                    .then_inc(h_ready, 1)

            def rotate(block, n, turn):
                t = 2 * (n % 2)
                pool.wait_ge(gu_taken, (block.gu + (2 * n + 2)).at(turn))
                pool.tensor_tensor(tmp[:, t, :], tmp[:, t, :], tmp[:, t + 1, :], ALU.add).then_inc(rot_sum, 1)
                pool.wait_ge(rot_high, (block.seq * 4 + (n + 1)).at(turn))
                pool.tensor_tensor(src[:, 1, n // 2, 1, n % 2, :], tmp[:, t, :], src[:, 1, n // 2, 0, n % 2, :], ALU.subtract)\
                    .then_inc(rot_ready, 1)

            def slot(s, turn):
                for tick in range(-1, TICKS):
                    for kind, n, block in s.steps(tick):
                        if kind == "N1":
                            rsqrt(block, turn)
                        elif kind == "N5" and block.name != "F":
                            add_bias(block, turn)
                        elif kind == "J":
                            ffn_step(block, n, turn)
                        elif kind == "W2":
                            rotate(block, n, turn)

            slot(first[0], 0)
            pool.wait_ge(wb_split, 1)
            pool.memset(k_pack(0).rearrange("p n s -> p (n s)").bitcast(F32), 0.0).then_inc(cleared, 1)
            slot(first[1], 0)
            with pool.Fori(0, SEQS // 2 - 1) as turn:
                for s in body:
                    slot(s, turn)
            for s in tail:
                slot(s, SEQS // 2 - 1)


def shape_constants():
    i = np.arange(DH // 2, dtype=np.float32)
    theta = np.power(np.float32(10000.0), np.float32(-2.0) * (i - np.float32(1.0)) / np.float32(DH)).astype(np.float32)
    angle = (np.arange(S, dtype=np.float32)[:, None] * theta[None, :]).astype(np.float32)
    d = np.arange(P) % DH
    cos = np.cos(angle)[:, d // 2].T
    sin = np.sin(angle)[:, d // 2].T * np.where(d % 2, 1.0, -1.0)[:, None]
    r = np.arange(P)[:, None]
    masks = []
    for t in (0, 3, 1, 2):
        a, b = WINDOW[t]
        near = np.abs(r + t * P - np.arange(a, b)[None, :]) <= HALF
        if t:
            near = np.concatenate([near, np.ones((P, GLOBALS), bool)], 1)
        else:
            near = (near | (np.arange(a, b)[None, :] < GLOBALS)) & (r >= GLOBALS)
        masks.append(np.where(near, 0.0, MASKED))
    masks.append(np.where(r <= np.arange(P)[None, :], 0.0, MASKED))
    masks.append(np.eye(P))
    masks.append(np.tile(np.where(np.arange(P) % 32 < GLOBALS, 0.0, MASKED), (P, 1)))
    masks.append(np.ones((P, 1)))
    masks.append(r % 32 == np.arange(GLOBALS)[None, :])
    strip = r // 32 == np.arange(HEADS)[None, :] % 4
    sel = (np.arange(2 * HEADS)[:, None] % HEADS == np.arange(HEADS)[None, :])
    f = lambda a, t: np.ascontiguousarray(a, dtype=t)
    bf16 = lambda a: np.ascontiguousarray(f(a, np.float32).view(np.uint32) >> 16, dtype=np.uint16)
    return {"cos": f(cos, np.float32), "sin": f(sin, np.float32),
            "masks": bf16(np.concatenate(masks, 1)), "eye": f(np.eye(P), np.float32),
            "sel": bf16(sel), "swap": f(np.eye(P)[np.arange(P) ^ 1], np.float16),
            "strip": f(strip, np.float32)}


_INS = ["L0_attn_a_x", "L0_attn_a_Wq", "L0_attn_a_bq", "L0_attn_a_Wk", "L0_attn_a_bk", "L0_attn_a_Wv", "L0_attn_a_bv",
        "L0_attn_a_Wo", "L0_attn_a_bo", "L0_attn_b_Wqkv", "L0_attn_b_Wout", "L0_attn_b_bout", "L0_ffn_w_gate",
        "L0_ffn_w_up", "L0_ffn_w_down"]


def kernel(**inputs):
    import numpy as _np
    import concourse.bacc as _bacc
    from concourse import mybir as _mybir
    from concourse.bass_utils import run_bass_kernel_spmd as _run

    nc = _bacc.Bacc("TRN2", target_bir_lowering=False, num_devices=1)
    arrays, args = {}, []
    given = {n: _np.ascontiguousarray(inputs[n]) for n in _INS}
    for name, a in {**given, **shape_constants()}.items():
        arrays[f"in_{name}_dram"] = a
        args.append(nc.dram_tensor(f"in_{name}_dram", a.shape, _mybir.dt.from_np(a.dtype), kind="ExternalInput").ap())
    args.append(nc.dram_tensor("out_dram", (SEQS, S, D), _mybir.dt.float32, kind="ExternalOutput").ap())
    build(nc, *args)
    r = _run(nc, [arrays], core_ids=[0])
    return r.results[0]["out_dram"]
```
